# Optimizing a Trainium2 kernel written in Bass

```python
import numpy as np
import jax
import jax.numpy as jnp

def _softmax(x, axis=-1):
    return jax.nn.softmax(x, axis=axis)

def _gelu(x):
    return jax.nn.gelu(x, approximate=True)

def _silu(x):
    return jax.nn.silu(x)

def _sigmoid(x):
    return jax.nn.sigmoid(x)

def _layernorm(x, axis=-1, eps=1e-05):
    m = jnp.mean(x, axis=axis, keepdims=True)
    v = jnp.var(x, axis=axis, keepdims=True)
    return (x - m) / jnp.sqrt(v + eps)

def _scatter_add(tgt, idx, src, axis=0):
    return tgt.at[idx].add(src)

def _segment_sum(src, seg, n):
    return jax.ops.segment_sum(src, seg, n)
kernel_name = 'mk_sandwich_d1_jaxref_r8_5a1ea3'

def setup_inputs(seed: int=0):
    np.random.seed(seed)
    _w = jnp.asarray

    def _L0_attn_setup():
        import jax, jax.numpy as jnp
        import numpy as np
        NUM_HEADS = 16
        DIM_HEAD = 64
        SCALE = DIM_HEAD ** (-0.5)
        ROPE_BASE = 10000.0

        def _rope(t):
            n, d = (t.shape[2], t.shape[3])
            inv_freq = 1.0 / ROPE_BASE ** (jnp.arange(0, d, 2, dtype=jnp.float32) / d)
            freqs = jnp.arange(n, dtype=jnp.float32)[:, None] * inv_freq[None, :]
            cos = jnp.concatenate([jnp.cos(freqs), jnp.cos(freqs)], axis=-1)
            sin = jnp.concatenate([jnp.sin(freqs), jnp.sin(freqs)], axis=-1)
            t1, t2 = jnp.split(t, 2, axis=-1)
            rot = jnp.concatenate([-t2, t1], axis=-1)
            return t * cos + rot * sin
        key = jax.random.key(seed)
        k1, k2, k3 = jax.random.split(key, 3)
        B, N, D = (2, 2049, 128)
        x = jax.random.normal(k1, (B, N, D), dtype=jnp.float32)
        ln_gamma = jnp.ones((D,), dtype=jnp.float32)
        ln_beta = jnp.zeros((D,), dtype=jnp.float32)
        w_qkv = jax.random.normal(k2, (D, 3 * NUM_HEADS * DIM_HEAD), dtype=jnp.float32) * 0.02
        w_out = jax.random.normal(k3, (NUM_HEADS * DIM_HEAD, D), dtype=jnp.float32) * 0.02
        return {'x': x, 'ln_gamma': ln_gamma, 'ln_beta': ln_beta, 'w_qkv': w_qkv, 'w_out': w_out}
    _L0_attn_in = _L0_attn_setup()

    def _L0_ffn_setup():
        import jax, jax.numpy as jnp
        import numpy as np
        E, D, F = (8, 128, 512)
        B, S = (4, 256)

        def _layernorm(x, g, b, eps=1e-05):
            mu = jnp.mean(x, axis=-1, keepdims=True)
            var = jnp.var(x, axis=-1, keepdims=True)
            return (x - mu) * jax.lax.rsqrt(var + eps) * g + b
        key = jax.random.key(seed)
        ks = jax.random.split(key, 5)
        return {'input_features': jax.random.normal(ks[0], (B, S, D), jnp.float32), 'centroids': jax.random.normal(ks[1], (E, D), jnp.float32) * 0.1, 'ln_g': jnp.ones((E, D), jnp.float32), 'ln_b': jnp.zeros((E, D), jnp.float32), 'w1': jax.random.normal(ks[2], (E, F, D), jnp.float32) * (1.0 / np.sqrt(D).astype(np.float32)), 'b1': jnp.zeros((E, F), jnp.float32), 'w2': jax.random.normal(ks[3], (E, D, F), jnp.float32) * (1.0 / np.sqrt(F).astype(np.float32)), 'b2': jnp.zeros((E, D), jnp.float32)}
    _L0_ffn_in = _L0_ffn_setup()
    _d = {'L0_attn_x': _L0_attn_in['x'], 'L0_attn_ln_gamma': _L0_attn_in['ln_gamma'], 'L0_attn_ln_beta': _L0_attn_in['ln_beta'], 'L0_attn_w_qkv': _L0_attn_in['w_qkv'], 'L0_attn_w_out': _L0_attn_in['w_out'], 'L0_ffn_centroids': _L0_ffn_in['centroids'], 'L0_ffn_ln_g': _L0_ffn_in['ln_g'], 'L0_ffn_ln_b': _L0_ffn_in['ln_b'], 'L0_ffn_w1': _L0_ffn_in['w1'], 'L0_ffn_b1': _L0_ffn_in['b1'], 'L0_ffn_w2': _L0_ffn_in['w2'], 'L0_ffn_b2': _L0_ffn_in['b2']}
    _x0 = _d['L0_attn_x']
    _d['L0_attn_x'] = jax.random.normal(jax.random.fold_in(jax.random.key(seed), 1), (8, 512, 128), dtype=_x0.dtype)
    del _x0
    return _d

def reference(L0_attn_x, L0_attn_ln_gamma, L0_attn_ln_beta, L0_attn_w_qkv, L0_attn_w_out, L0_ffn_centroids, L0_ffn_ln_g, L0_ffn_ln_b, L0_ffn_w1, L0_ffn_b1, L0_ffn_w2, L0_ffn_b2):

    def _L0_attn_ref(x, ln_gamma, ln_beta, w_qkv, w_out):
        import jax, jax.numpy as jnp
        import numpy as np
        NUM_HEADS = 16
        DIM_HEAD = 64
        SCALE = DIM_HEAD ** (-0.5)
        ROPE_BASE = 10000.0

        def _rope(t):
            n, d = (t.shape[2], t.shape[3])
            inv_freq = 1.0 / ROPE_BASE ** (jnp.arange(0, d, 2, dtype=jnp.float32) / d)
            freqs = jnp.arange(n, dtype=jnp.float32)[:, None] * inv_freq[None, :]
            cos = jnp.concatenate([jnp.cos(freqs), jnp.cos(freqs)], axis=-1)
            sin = jnp.concatenate([jnp.sin(freqs), jnp.sin(freqs)], axis=-1)
            t1, t2 = jnp.split(t, 2, axis=-1)
            rot = jnp.concatenate([-t2, t1], axis=-1)
            return t * cos + rot * sin
        B, N, D = x.shape
        mu = jnp.mean(x, axis=-1, keepdims=True)
        var = jnp.mean(jnp.square(x - mu), axis=-1, keepdims=True)
        xn = (x - mu) * jax.lax.rsqrt(var + 1e-05) * ln_gamma + ln_beta
        qkv = xn @ w_qkv
        q, k, v = jnp.split(qkv, 3, axis=-1)

        def to_heads(t):
            return t.reshape(B, N, NUM_HEADS, DIM_HEAD).transpose(0, 2, 1, 3)
        q, k, v = (to_heads(q), to_heads(k), to_heads(v))
        q = jnp.concatenate([q[:, :, :1, :], _rope(q[:, :, 1:, :])], axis=2)
        k = jnp.concatenate([k[:, :, :1, :], _rope(k[:, :, 1:, :])], axis=2)
        dots = jnp.einsum('bhqd,bhkd->bhqk', q, k) * SCALE
        attn = jax.nn.softmax(dots, axis=-1)
        out = jnp.einsum('bhqk,bhkd->bhqd', attn, v)
        out = out.transpose(0, 2, 1, 3).reshape(B, N, NUM_HEADS * DIM_HEAD)
        return out @ w_out

    def _L0_ffn_ref(input_features, centroids, ln_g, ln_b, w1, b1, w2, b2):
        import jax, jax.numpy as jnp
        import numpy as np
        E, D, F = (8, 128, 512)
        B, S = (4, 256)

        def _layernorm(x, g, b, eps=1e-05):
            mu = jnp.mean(x, axis=-1, keepdims=True)
            var = jnp.var(x, axis=-1, keepdims=True)
            return (x - mu) * jax.lax.rsqrt(var + eps) * g + b
        Bf, Sf, Df = input_features.shape
        x = input_features.reshape(-1, Df)
        aff = x @ centroids.T
        assign = jnp.argmax(aff, axis=1)
        order = jnp.argsort(assign)
        xs = x[order]
        es = assign[order]
        alpha = jax.nn.sigmoid(jnp.take_along_axis(aff[order], es[:, None], axis=1))
        nE = centroids.shape[0]
        y = jnp.zeros_like(xs)
        for e in range(nE):
            h = _layernorm(xs, ln_g[e], ln_b[e])
            h = jax.nn.relu(h @ w1[e].T + b1[e])
            ye = xs + h @ w2[e].T + b2[e]
            y = y + jnp.where((es == e)[:, None], ye, 0.0)
        out_sorted = alpha * y + (1.0 - alpha) * xs
        inv = jnp.argsort(order)
        return out_sorted[inv].reshape(Bf, Sf, Df)
    x = L0_attn_x
    x = x + _layernorm(_L0_attn_ref(_layernorm(x, axis=-1), L0_attn_ln_gamma, L0_attn_ln_beta, L0_attn_w_qkv, L0_attn_w_out), axis=-1)
    x = x + _layernorm(_L0_ffn_ref(_layernorm(x, axis=-1), L0_ffn_centroids, L0_ffn_ln_g, L0_ffn_ln_b, L0_ffn_w1, L0_ffn_b1, L0_ffn_w2, L0_ffn_b2), axis=-1)
    return x

_drawn_inputs = setup_inputs


def setup_inputs(seed=0):
    import zlib

    import numpy as np

    out = dict(_drawn_inputs(seed))
    spreads = {'L0_attn_ln_gamma': (1.0, 0.2),
     'L0_attn_ln_beta': (0.0, 0.1),
     'L0_ffn_ln_g': (1.0, 0.2),
     'L0_ffn_ln_b': (0.0, 0.393),
     'L0_ffn_b1': (0.0, 0.403),
     'L0_ffn_b2': (0.0, 0.295)}
    factors = {}
    for name, (base, spread) in spreads.items():
        noise = np.random.default_rng([zlib.crc32(name.encode()), seed]).standard_normal(out[name].shape)
        drawn = base * np.exp(spread * noise) if base else spread * noise
        out[name] = jnp.asarray(drawn.astype(out[name].dtype))
    for name, factor in factors.items():
        out[name] = (out[name] * factor).astype(out[name].dtype)
    return out
```

```python
from contextlib import ExitStack

import numpy as np

import concourse.bass as bass
from concourse import mybir

F32 = mybir.dt.float32
F32R = mybir.dt.float32r
I32 = mybir.dt.int32
U32 = mybir.dt.uint32
ALU = mybir.AluOpType
ACT = mybir.ActivationFunctionType
AX = mybir.AxisListType

B, N, D = 8, 512, 128
H, DH = 16, 64
E, F = 8, 512
P = 128
EPS = 1e-5
SCALE = DH ** -0.5

NP = H // 2
PAIRS = B * NP
KT = N // P
TILES = B * KT
HALF = DH // 2
WC = 2 * P
FC = F // P
AHEAD = 6
BEHIND = 5
RING = 2 * KT

SLOTS = TILES + E - 1
CAP = B * N + P
ROWS = E * CAP + P
XH, XS, X1, ALPHA, REST, TOKEN, ROW = 0, D, 2 * D, 3 * D, 3 * D + 1, 3 * D + 2, 3 * D + 4
NO_TOKEN = 1 << 20


def sandwich_program(nc, x, wqk, wv, wo, rope, gb, cent_t, eg, eb, w1t, b1, w2t, b2, out):
    rows = nc.dram_tensor("rows", (ROWS, ROW), F32, kind="Internal").ap()
    den_row = nc.dram_tensor("den_row", (2, N), F32, kind="Internal").ap()
    rden_row = nc.dram_tensor("rden_row", (2, N), F32, kind="Internal").ap()

    ctx = ExitStack()
    with ctx:
        def sem(name):
            return ctx.enter_context(nc.semaphore(name))

        def keep(name, shape, dt=F32):
            return ctx.enter_context(nc.sbuf_tensor(name, shape, dt))

        acc = keep("acc", [P, RING, D])
        ident = keep("ident", [P, P])
        ones = keep("ones", [P, P])
        upper = keep("upper", [P, P])
        nothing = keep("nothing", [P, D])
        gbs = keep("gbs", [P, 2])
        minus_half = keep("minus_half", [P, 1])
        eps = keep("eps", [P, 1])
        w1s = keep("w1s", [P, E, F])
        w2s = keep("w2s", [P, E, FC, D])
        egb = keep("egb", [P, 2, E])
        cts = keep("cts", [P, E])
        pay = keep("pay", [P, BEHIND, ROW])
        xq = keep("xq", [P, BEHIND, D])
        tmp = keep("tmp", [P, BEHIND, D])
        xst = keep("xst", [P, BEHIND, D])
        stats = keep("stats", [P, BEHIND, 8])
        rstd_q = keep("rstd_q", [P, BEHIND, 2])
        rt = keep("rt", [P, BEHIND, 8])
        ra = keep("ra", [P, BEHIND, 2, E])
        oh = keep("oh", [P, BEHIND, E])
        pos = keep("pos", [P, BEHIND], U32)
        base = keep("base", [P, E])
        token = keep("token", [P, 1])
        iota8 = keep("iota8", [P, E])
        first_row = keep("first_row", [P, E])
        iota128 = keep("iota128", [P, TILES])
        iotas = keep("iotas", [P, SLOTS])
        part = keep("part", [P, 1])

        attn = ExitStack()

        def at(name, shape, dt=F32):
            return attn.enter_context(nc.sbuf_tensor(name, shape, dt))

        probs = at("probs", [P, 2, 2, KT, N])
        psums = at("psums", [P, 2, 2, N])
        xt_hi = at("xt_hi", [P, RING * P], F32R)
        xt_lo = at("xt_lo", [P, RING * P], F32R)
        xt = at("xt", [P, RING * P])
        wqk_all = at("wqk_all", [P, NP, 2 * WC], F32R)
        wqk_st = at("wqk_st", [P, 2, 2 * WC], F32R)
        wv_st = at("wv_st", [P, 2, 2 * DH])
        wo_st = at("wo_st", [P, 2, D])
        xt_st = at("xt_st", [P, N])
        kk = at("kk", [P, 2, 2, 2, N], F32R)
        qq = at("qq", [P, 2, 2, 2, N], F32R)
        vals = at("vals", [P, 2, KT, 2 * DH])
        rope_c = at("rope_c", [P, 2, N])
        rope_s = at("rope_s", [P, 2, N])
        rope_w = at("rope_w", [P, 2, N])
        roped = at("roped", [P, 2, N])
        cs = at("cs", [P, 3, N])
        mxp = at("mxp", [P, P])
        osb = at("osb", [P, 2, N])
        den_sb = at("den_sb", [P, N])
        den8 = at("den8", [P, 8])
        rden8 = at("rden8", [P, 8])
        rden = at("rden", [P, N])
        onorm = at("onorm", [P, N])
        xraw = at("xraw", [P, D])
        xn = at("xn", [P, 2, D])
        pst = at("pst", [P, 8])
        prs = at("prs", [P, 2])
        w_land = psums[:, :].rearrange("p r h (a n) -> p (r h a) n", n=WC)
        attn.close()

        ffn = ExitStack()

        def ff(name, shape, dt=F32):
            return ffn.enter_context(nc.sbuf_tensor(name, shape, dt))

        b1s = ff("b1s", [P, E, F])
        b2s = ff("b2s", [P, E, D])
        cmp = ff("cmp", [P, E, TILES])
        ex = ff("ex", [P, 6, E])
        sa = ff("sa", [P, 2, SLOTS, E])
        sl = ff("sl", [P, 4, SLOTS])
        texp = ff("texp", [P, SLOTS], I32)
        tdest = ff("tdest", [P, SLOTS], I32)
        fill = ff("fill", [P, ROW])
        fpos = ff("fpos", [P, E], U32)
        NB = 4
        xh_in = ff("xh_in", [P, NB, D])
        rest_in = ff("rest_in", [P, NB, ROW - XS])
        tok = ff("tok", [P, NB], U32)
        xte = ff("xte", [P, NB, P])
        hrow = ff("hrow", [P, NB, F])
        hcol = ff("hcol", [P, NB, FC, P])
        yrow = ff("yrow", [P, NB, D])
        fst = ff("fst", [P, NB, 8])
        frs = ff("frs", [P, NB, 2])
        ores = ff("ores", [P, NB, D])
        ffn.close()

        bank = [ctx.enter_context(nc.psum_tensor(f"bank{i}", [P, 512], F32)) for i in range(4)]
        st_ps = ctx.enter_context(nc.psum_tensor("st_ps", [P, 2, N], F32))
        mx_ps = ctx.enter_context(nc.psum_tensor("mx_ps", [P, 2, N], F32))
        scr0, scr1, o_ps, aux_ps = bank
        z_ps = [ps[:, h, 0:D] for ps in (mx_ps, st_ps) for h in range(2)]

        s_const = sem("s_const")
        s_w = [sem(f"s_w{i}") for i in range(NP)]
        s_whi = sem("s_whi")
        s_wlo = sem("s_wlo")
        s_gconst = sem("s_gconst")
        s_gc = sem("s_gc")
        s_clear = sem("s_clear")
        s_ew = sem("s_ew")

        x_in = sem("x_in")
        p_v = sem("p_v")
        p_stat = sem("p_stat")
        p_rstd = sem("p_rstd")
        p_g = sem("p_g")
        p_tr = sem("p_tr")
        p_xt = sem("p_xt")
        p_hi = sem("p_hi")
        p_lo = sem("p_lo")

        qk_in = [sem("qk_in0"), sem("qk_in1")]
        wv_in = [sem("wv_in0"), sem("wv_in1")]
        xt_in = sem("xt_in")
        wo_in = [sem("wo_in0"), sem("wo_in1")]
        qk_proj = sem("qk_proj")
        v_proj = sem("v_proj")
        rope_read = sem("rope_read")
        swap_in = sem("swap_in")
        rope_added = sem("rope_added")
        hi_done = sem("hi_done")
        lo_done = sem("lo_done")
        v_read = sem("v_read")
        max_mm = sem("max_mm")
        max_read = sem("max_read")
        t_done = sem("t_done")
        mask_done = sem("mask_done")
        st_mm = sem("st_mm")
        exp_done = sem("exp_done")
        av_done = sem("av_done")
        o_copied = sem("o_copied")
        pool_sum = sem("pool_sum")
        den_mm = sem("den_mm")
        den_copied = sem("den_copied")
        den_out = sem("den_out")
        den8_in = sem("den8_in")
        den_recip = sem("den_recip")
        rden_out = sem("rden_out")
        rden_in = sem("rden_in")
        o_norm = sem("o_norm")
        out_mm = sem("out_mm")
        out_read = sem("out_read")

        q_in = sem("q_in")
        q_v = sem("q_v")
        q_stat = sem("q_stat")
        q_rstd = sem("q_rstd")
        q_g = sem("q_g")
        q_xs = sem("q_xs")
        q_xst = sem("q_xst")
        q_xsc = sem("q_xsc")
        q_aff = sem("q_aff")
        q_mx = sem("q_mx")
        q_ea = sem("q_ea")
        q_oh = sem("q_oh")
        q_rank = sem("q_rank")
        q_route = sem("q_route")
        q_scat = sem("q_scat")

        s_eb = sem("s_eb")
        s_route = sem("s_route")
        r_v = sem("r_v")
        r_p = sem("r_p")
        s_fill = sem("s_fill")
        s_dummy = sem("s_dummy")
        fin = [sem(f"fin{i}") for i in range(NB)]
        frest = [sem(f"frest{i}") for i in range(NB)]
        ft = [sem(f"ft{i}") for i in range(NB)]
        fxt = [sem(f"fxt{i}") for i in range(NB)]
        fh = [sem(f"fh{i}") for i in range(NB)]
        fhb = [sem(f"fhb{i}") for i in range(NB)]
        fht = [sem(f"fht{i}") for i in range(NB)]
        fhr = [sem(f"fhr{i}") for i in range(NB)]
        fz = [sem(f"fz{i}") for i in range(NB)]
        fzr = [sem(f"fzr{i}") for i in range(NB)]
        f_v = sem("f_v")
        f_stat = sem("f_stat")
        f_rstd = sem("f_rstd")
        f_g = sem("f_g")
        f_bn = sem("f_bn")
        f_norm = sem("f_norm")
        f_tok = sem("f_tok")
        f_res = sem("f_res")
        fout = [sem(f"fout{i}") for i in range(NB)]

        Q_STEPS = 15
        F_STEPS = 3

        def ge(eng, s, v):
            if isinstance(v, int) and v <= 0:
                return
            eng.wait_ge(s, v)

        def pairs(eng, body):
            body(0, True, False)
            body(1, True, False)
            with eng.Fori(2, BEHIND) as m:
                body(m, True, False)
            body(BEHIND, True, True)
            with eng.Fori(BEHIND + 1, TILES - AHEAD) as m:
                body(m, True, True)
            with eng.Fori(TILES - AHEAD, TILES - 2) as m:
                body(m, False, True)
            body(TILES - 2, False, True)
            body(TILES - 1, False, True)

        def m_is(m, value):
            return isinstance(m, int) and m == value

        def batch(m):
            return m // KT

        def slots(eng, step):
            def one(t, u):
                step(t, u % NB, lambda d: not isinstance(t, int) or 0 <= t + d < SLOTS)
            end = (SLOTS - NB) // NB
            for t in range(-3, NB + 1):
                one(t, t % NB)
            with eng.Fori(1, end) as m:
                for i in range(1, NB + 1):
                    one(NB * m + i, i % NB)
            for t in range(NB * end + 1, SLOTS + 3):
                one(t, t % NB)

        def turn(t, u):
            return t // NB if isinstance(t, int) else (t - u) // NB

        x_t = x.rearrange("b n d -> (b n) d").rearrange("(t p) d -> t p d", p=P)
        out_rows = out.rearrange("b n d -> (b n) d")

        block = ctx.enter_context(nc.Block())

        @block.sync
        def _(sp):
            def load_x(T):
                ge(sp, p_v, 4 * T - 2)
                src = x_t[T] if isinstance(T, int) else x_t[bass.ds(T, 1)].rearrange("o p d -> p (o d)")
                sp.dma_start(xraw[:, :], src).then_inc(x_in, 16)

            load_x(0)
            sp.dma_start(cs[:, :, :], rope.rearrange("c p n -> p c n")).then_inc(s_const, 16)
            sp.dma_start(gbs[:, :], gb).then_inc(s_const, 16)
            for p in range(NP):
                sp.dma_start(w_land[:, p, :], wqk[p]).then_inc(s_w[p], 16)
            for T in range(1, AHEAD):
                load_x(T)

            def stage_qk(j, r, p):
                ge(sp, qk_proj, 2 * j - 2)
                sp.dma_start(wqk_st[:, r, :].bitcast(F32), wqk_all[:, p, :].bitcast(F32)).then_inc(qk_in[r], 16)

            def stage_v(j, r, p):
                ge(sp, v_proj, j - 1)
                sp.dma_start(wv_st[:, r, :], wv[p]).then_inc(wv_in[r], 16)

            def stage_out(j, r, p):
                ge(sp, out_mm, j - 1)
                sp.dma_start(wo_st[:, r, :], wo[p]).then_inc(wo_in[r], 16)

            def stage_x(m):
                ge(sp, v_proj, 2 * m)
                sp.wait_ge(p_xt, KT * batch(m) + KT)
                sp.dma_start(xt_st[:, :], xt[:, bass.ds(batch(m) % 2 * N, N)]).then_inc(xt_in, 16)

            def swap(j):
                sp.wait_ge(rope_read, 4 * j + 4)
                for q in range(4):
                    to, fr = q * HALF, (q ^ 1) * HALF
                    sp.dma_start(rope_w[to:to + HALF, :, :], rope_s[fr:fr + HALF, :, :]).then_inc(swap_in, 16)

            def den_spread(n):
                sp.wait_ge(den_copied, n + 1)
                for h in range(2):
                    sp.dma_start(den_row[h:h + 1, :], den_sb[h * DH:h * DH + 1, :]).then_inc(den_out, 16)
                sp.wait_ge(den_out, 32 * (n + 1))
                sp.dma_start(den8[:, :], den_row.rearrange("h (p c) -> (h p) c", c=8)).then_inc(den8_in, 16)

            def rden_spread(n):
                ge(sp, o_norm, n)
                sp.wait_ge(den_recip, n + 1)
                sp.dma_start(rden_row.rearrange("h (p c) -> (h p) c", c=8), rden8[:, :]).then_inc(rden_out, 16)
                sp.wait_ge(rden_out, 16 * (n + 1))
                for h in range(2):
                    sp.dma_start(rden[h * DH:(h + 1) * DH, :], rden_row[h:h + 1, :].to_broadcast([DH, N])).then_inc(rden_in, 16)

            def load_q(Q):
                ge(sp, q_stat, 3 * Q - 1)
                sp.dma_start(xq[:, 0, :], x_t[bass.ds(Q, 1)].rearrange("o p d -> p (o d)")).then_inc(q_in, 16)

            def body(m, prep, post):
                first = isinstance(m, int) and m == 0
                last = isinstance(m, int) and m == TILES - 1
                half = NP // 2
                for r in range(2):
                    n = 2 * m + r
                    if not r and prep:
                        load_x(m + AHEAD)
                    if not r and post:
                        load_q(m - BEHIND)
                    if not m_is(m, TILES - 2) and not last:
                        stage_qk(n + 4, r, (m + 2) % half * 2 + r)
                    if not (first and not r):
                        den_spread(n - 1)
                    if not r and not last:
                        stage_x(m + 1)
                    if not (last or m_is(m, TILES - 2) and r):
                        stage_v(n + 3, 1 - r, (m + 1 + r) % half * 2 + 1 - r)
                    if not first:
                        stage_out(n - 1, 1 - r, (m + r - 1) % half * 2 + 1 - r)
                    if not (first and not r):
                        rden_spread(n - 1)
                    if not (last or m_is(m, TILES - 2) and r):
                        swap(n + 3)

            for n in (0, 1):
                sp.wait_ge(s_whi, n + 1)
                sp.wait_ge(s_wlo, n + 1)
                stage_qk(n, n, n)
            stage_x(0)
            for n in (0, 1):
                stage_v(n, n, n)
                stage_out(n, n, n)
            swap(0)
            for n in (2, 3):
                sp.wait_ge(s_whi, NP)
                sp.wait_ge(s_wlo, NP)
                stage_qk(n, n - 2, n)
                if n == 2:
                    swap(1)
                    stage_v(2, 0, 2)
            swap(2)
            sp.dma_start(w1s[:, :, :], w1t.rearrange("e d f -> d e f")).then_inc(s_ew, 16)
            sp.dma_start(w2s[:, :, :, :], w2t.rearrange("e (c p) d -> p e c d", p=P)).then_inc(s_ew, 16)
            sp.dma_start(egb[:, 0, :], eg).then_inc(s_ew, 16)
            sp.dma_start(egb[:, 1, :], eb).then_inc(s_ew, 16)
            sp.dma_start(cts[:, :], cent_t).then_inc(s_ew, 16)
            pairs(sp, body)
            den_spread(PAIRS - 1)
            stage_out(PAIRS - 1, 1, NP - 1)
            sp.wait_ge(q_stat, 3 * (TILES - BEHIND) - 1)
            for k in range(BEHIND):
                sp.dma_start(xq[:, k, :], x_t[TILES - BEHIND + k]).then_inc(q_in, 16)
            rden_spread(PAIRS - 1)

            sp.wait_ge(out_read, PAIRS)
            sp.dma_start(b1s[:, :, :], b1.rearrange("(o e) f -> o e f", o=1).to_broadcast([P, E, F])).then_inc(s_eb, 16)
            sp.dma_start(b2s[:, :, :], b2.rearrange("(o e) f -> o e f", o=1).to_broadcast([P, E, D])).then_inc(s_eb, 16)
            sp.wait_ge(r_p, 2)
            sp.dma_start(rows[E * CAP:ROWS, :], fill[:, :]).then_inc(s_dummy, 16)
            sp.wait_ge(s_route, 1)
            sp.wait_ge(q_scat, 16 * TILES)
            sp.wait_ge(s_dummy, 16)
            sp.wait_ge(s_fill, 16 * E)

            def step(t, u, on):
                if on(3):
                    w = (u + 3) % NB
                    at_row = sp.value_load(tdest[0:1, bass.ds(t + 3, 1)], min_val=0, max_val=E * CAP)
                    ge(sp, ft[w], turn(t + 3, w))
                    sp.dma_start(xh_in[:, w, :], rows[bass.ds(at_row, P), XH:XH + D]).then_inc(fin[w], 16)
                if on(1):
                    w = (u + 1) % NB
                    at_row = sp.value_load(tdest[0:1, bass.ds(t + 1, 1)], min_val=0, max_val=E * CAP)
                    ge(sp, fout[w], 16 * turn(t + 1, w))
                    sp.dma_start(rest_in[:, w, :], rows[bass.ds(at_row, P), XS:ROW]).then_inc(frest[w], 16)

            slots(sp, step)
            for u in range(NB):
                sp.wait_ge(fout[u], 16 * ((SLOTS - u + NB - 1) // NB))

        @block.gpsimd
        def _(pool):
            g = nc.gpsimd
            order = [0]

            def link(ins):
                order[0] += 1
                ins.then_inc(s_gc, 1)
                pool.wait_ge(s_gc, order[0])

            g.memset(ident[:, :], 0.0)
            g.memset(upper[:, :], 1.0)
            g.memset(minus_half[:, :], -0.5)
            g.memset(eps[:, :], EPS)
            g.memset(nothing[:, :], 0.0)
            g.memset(mxp[:, :], 0.0)
            link(g.memset(ones[:, :], 1.0))
            g.affine_select(out=ident[:, :], in_=ident[:, :], compare_op=ALU.not_equal, fill=1.0,
                            base=0, pattern=[[-1, P]], channel_multiplier=1)
            g.affine_select(out=upper[:, :], in_=upper[:, :], compare_op=ALU.is_gt, fill=0.0,
                            base=0, pattern=[[1, P]], channel_multiplier=-1)

            def iota(ap, step, cm=0, base_=0):
                return g.iota(ap, [[step, ap.shape[-1]]], base=base_, channel_multiplier=cm,
                              allow_small_or_imprecise_dtypes=True)

            iota(iota8[:, :], 1)
            iota(first_row[:, :], CAP)
            iota(base[:, :], CAP)
            iota(iota128[:, :], P)
            iota(iotas[:, :], 1)
            iota(token[:, :], 1, cm=1)
            iota(part[:, :], 1, cm=1).then_inc(s_gconst, 1)

            def rstd(src, dst, stat, own, done, i):
                pool.wait_ge(stat, i + 1)
                g.tensor_tensor(dst, src, eps[:, :], ALU.add).then_inc(own, 1)
                pool.wait_ge(own, i + 1)
                g.tensor_tensor(dst, dst, minus_half[:, :], ALU.pow).then_inc(done, 1)

            def p_rs(T, i):
                rstd(pst[:, 7:8], prs[:, i:i + 1], p_stat, p_g, p_rstd, 2 * T + i)

            def q_rs(Q, i, k=0):
                rstd(stats[:, k, 7:8], rstd_q[:, k, 0:1], q_stat, q_g, q_rstd, Q * 3 + i)

            def low_x(T):
                pool.wait_ge(p_hi, T + 1)
                at_ = bass.ds(T % RING * P, P)
                g.tensor_tensor(xt_lo[:, at_], xt[:, at_], xt_hi[:, at_].bitcast(F32), ALU.subtract).then_inc(p_lo, 1)

            def low_weights(p):
                pool.wait_ge(s_whi, p + 1)
                g.tensor_tensor(wqk_all[:, p, WC:2 * WC], w_land[:, p, :], wqk_all[:, p, 0:WC].bitcast(F32),
                                ALU.subtract).then_inc(s_wlo, 1)

            for T in range(AHEAD):
                p_rs(T, 0)
                p_rs(T, 1)
                low_x(T)
                if T < 2:
                    low_weights(T)
            for p in range(2, NP):
                low_weights(p)

            def add_rope(j):
                pool.wait_ge(swap_in, 64 * (j + 1))
                ge(pool, hi_done, 6 * j)
                ge(pool, lo_done, 4 * j)
                g.tensor_tensor(roped[:, :, :], rope_c[:, :, :], rope_w[:, :, :], ALU.add).then_inc(rope_added, 1)

            def add_probs(n, r, kt):
                if kt == 1:
                    ge(pool, den_mm, n - 1)
                else:
                    pool.wait_ge(pool_sum, 3 * n + kt - 1)
                pool.wait_ge(exp_done, 8 * n + 2 * kt + 2)
                first = probs[:, r, :, 0, :] if kt == 1 else psums[:, r, :, :]
                g.tensor_tensor(psums[:, r, :, :], first, probs[:, r, :, kt, :], ALU.add).then_inc(pool_sum, 1)

            def normalise(n, r):
                pool.wait_ge(rden_in, 32 * (n + 1))
                pool.wait_ge(o_copied, n + 1)
                ge(pool, out_mm, n)
                g.tensor_tensor(onorm[:, :], osb[:, r, :], rden[:, :], ALU.mult).then_inc(o_norm, 1)

            def scatter(k=0):
                g.indirect_dma_start(out=rows, out_offset=bass.IndirectOffsetOnAxis(ap=pos[:, k:k + 1], axis=0),
                                     in_=pay[:, k, :], in_offset=None).then_inc(q_scat, 16)

            def body(m, prep, post):
                first = isinstance(m, int) and m == 0
                last = isinstance(m, int) and m == TILES - 1
                T, Q = m + AHEAD, m - BEHIND
                for r in range(2):
                    n = 2 * m + r
                    if not first:
                        normalise(n - 2, r)
                    scattered = not r and post and not m_is(m, BEHIND)
                    if scattered:
                        pool.wait_ge(q_route, Q)
                    if not last:
                        add_rope(n + 2)
                    elif scattered:
                        add_probs(n, r, 1)
                    if scattered:
                        scatter()
                    if not r and prep:
                        p_rs(T, 0)
                    if not r and post:
                        q_rs(Q, 0)
                    if not (last and scattered):
                        add_probs(n, r, 1)
                    if not r and post:
                        q_rs(Q, 1)
                    if not r and prep:
                        p_rs(T, 1)
                    if r and prep:
                        low_x(T)
                    add_probs(n, r, 2)
                    if not r and post:
                        q_rs(Q, 2)
                    add_probs(n, r, 3)

            add_rope(0)
            add_rope(1)
            pairs(pool, body)
            pool.wait_ge(q_route, TILES - BEHIND)
            scatter()
            normalise(PAIRS - 2, 0)
            normalise(PAIRS - 1, 1)
            for i in range(3):
                for k in range(BEHIND):
                    pool.wait_ge(q_stat, 3 * (TILES - BEHIND) + i * BEHIND + k + 1)
                    g.tensor_tensor(rstd_q[:, k, 0:1], stats[:, k, 7:8], eps[:, :], ALU.add).then_inc(q_g, 1)
                    pool.wait_ge(q_g, 3 * (TILES - BEHIND) + i * BEHIND + k + 1)
                    g.tensor_tensor(rstd_q[:, k, 0:1], rstd_q[:, k, 0:1], minus_half[:, :], ALU.pow).then_inc(q_rstd, 1)
            for k in range(BEHIND):
                pool.wait_ge(q_route, TILES - BEHIND + k + 1)
                scatter(k)
            pool.wait_ge(out_read, PAIRS)
            g.memset(fill[:, :], 0.0).then_inc(r_p, 1)
            pool.wait_ge(r_p, 1)
            g.memset(fill[:, TOKEN:TOKEN + 1], float(NO_TOKEN)).then_inc(r_p, 1)
            pool.wait_ge(r_p, 2)
            pool.wait_ge(s_route, 1)
            for e in range(E):
                g.indirect_dma_start(out=rows, out_offset=bass.IndirectOffsetOnAxis(ap=fpos[:, e:e + 1], axis=0),
                                     in_=fill[:, :], in_offset=None).then_inc(s_fill, 16)

            def step(t, u, on):
                if on(-3):
                    pool.wait_ge(f_res, t - 2)
                    pool.wait_ge(f_tok, t - 2)
                if on(-1):
                    w = (u - 1) % NB
                    pool.wait_ge(f_stat, t)
                    g.tensor_tensor(frs[:, w, 0:1], fst[:, w, 7:8], eps[:, :], ALU.add).then_inc(f_g, 1)
                    pool.wait_ge(f_g, t)
                    g.tensor_tensor(frs[:, w, 0:1], frs[:, w, 0:1], minus_half[:, :], ALU.pow).then_inc(f_rstd, 1)
                if on(-3):
                    w = (u - 3) % NB
                    g.indirect_dma_start(out=out_rows, out_offset=bass.IndirectOffsetOnAxis(ap=tok[:, w:w + 1], axis=0),
                                         in_=ores[:, w, :], in_offset=None, bounds_check=B * N - 1,
                                         oob_is_err=False).then_inc(fout[w], 16)
                if on(-2):
                    w = (u - 2) % NB
                    pool.wait_ge(f_norm, t - 1)
                    g.tensor_tensor(ores[:, w, :], yrow[:, w, :], rest_in[:, w, X1 - XS:X1 - XS + D], ALU.add)\
                     .then_inc(f_res, 1)

            slots(pool, step)

        @block.scalar
        def _(act):
            a = nc.scalar

            def high_weights(p):
                act.wait_ge(s_w[p], 16)
                a.activation(wqk_all[:, p, 0:WC], w_land[:, p, :], ACT.Copy).then_inc(s_whi, 1)

            def high_x(T):
                act.wait_ge(p_xt, T + 1)
                at_ = bass.ds(T % RING * P, P)
                a.activation(xt_hi[:, at_], xt[:, at_], ACT.Copy).then_inc(p_hi, 1)

            for T in range(AHEAD):
                if T < 2:
                    high_weights(T)
                high_x(T)
            for p in range(2, NP):
                high_weights(p)

            def copy_v(j, r):
                act.wait_ge(v_proj, j + 1)
                ge(act, av_done, j - 1)
                a.activation(vals[:, r].rearrange("p k d -> p (k d)"), scr0[:, :], ACT.Copy).then_inc(v_read, 1)

            def copy_o(n, r):
                act.wait_ge(av_done, n + 1)
                ge(act, o_norm, n - 1)
                a.activation(osb[:, r, :], o_ps[:, :], ACT.Copy).then_inc(o_copied, 1)

            def copy_den(n):
                act.wait_ge(den_mm, n + 1)
                ge(act, den_out, 32 * n)
                a.activation(den_sb[:, :], aux_ps[:, :], ACT.Copy).then_inc(den_copied, 1)

            def split_q(j, r):
                act.wait_ge(rope_added, j + 1)
                ge(act, st_mm, 8 * (j - 1))
                for h in range(2):
                    src = roped[h * DH:(h + 1) * DH, 0, :]
                    a.activation(qq[0:DH, r, 0, h, :], src, ACT.Copy).then_inc(hi_done, 1)
                    a.activation(qq[DH:P, r, 0, h, :], src, ACT.Copy).then_inc(hi_done, 1)

            def split_k(j, r):
                for h in range(2):
                    half = slice(h * DH, (h + 1) * DH)
                    for c in range(2):
                        ins = a.activation(kk[half, r, c, h, :], roped[half, 1, :], ACT.Copy)
                    ins.then_inc(hi_done, 1)

            def exps(n, r, kt):
                for h in range(2):
                    act.wait_ge(st_mm, 8 * n + 2 * kt + h + 1)
                    if kt == 0 and h == 0:
                        ge(act, av_done, n - 1)
                        ge(act, pool_sum, 3 * (n - 1))
                    a.activation(probs[:, r, h, kt, :], st_ps[:, h, :], ACT.Exp, scale=SCALE).then_inc(exp_done, 1)

            def exp_alpha(Q, k=0):
                act.wait_ge(q_mx, Q + 1)
                a.activation(rt[:, k, 1:2], rt[:, k, 0:1], ACT.Exp, scale=-1.0).then_inc(q_ea, 1)

            def body(m, prep, post):
                first = isinstance(m, int) and m == 0
                last = isinstance(m, int) and m == TILES - 1
                for r in range(2):
                    n = 2 * m + r
                    more = not (last and r)
                    if not (first and not r):
                        copy_o(n - 1, 1 - r)
                    exps(n, r, 0)
                    if not (first and not r):
                        copy_den(n - 1)
                    if more:
                        copy_v(n + 1, 1 - r)
                    exps(n, r, 1)
                    if r and prep:
                        high_x(m + AHEAD)
                    exps(n, r, 2)
                    exps(n, r, 3)
                    if r and post:
                        exp_alpha(m - BEHIND)
                    if not last:
                        split_q(n + 2, r)
                        split_k(n + 2, r)

            split_q(0, 0)
            split_k(0, 0)
            copy_v(0, 0)
            split_q(1, 1)
            split_k(1, 1)
            pairs(act, body)
            copy_o(PAIRS - 1, 1)
            copy_den(PAIRS - 1)
            for k in range(BEHIND):
                exp_alpha(TILES - BEHIND + k, k)

            def step(t, u, on):
                if on(0):
                    act.wait_ge(fht[u], turn(t, u) + 1)
                    ge(act, fz[u], turn(t, u))
                    a.activation(hcol[:, u].rearrange("p c t -> p (c t)"), bank[u][:, :], ACT.Relu).then_inc(fhr[u], 1)

            slots(act, step)

        @block.vector
        def _(dve):
            v = nc.vector

            def stat(src, st, own):
                v.bn_stats(st[:, 0:6], src).then_inc(own, 1)

            def aggregate(st, done):
                v.bn_aggr(st[:, 6:8], st[:, 0:6]).then_inc(done, 1)

            def p_first(T):
                dve.wait_ge(x_in, 16 * (T + 1))
                ge(dve, p_rstd, 2 * T)
                stat(xraw[:, :], pst, p_v)

            def p_second(T):
                dve.wait_ge(p_rstd, 2 * T + 1)
                v.tensor_scalar(xn[:, 0, :], xraw[:, :], pst[:, 6:7], prs[:, 0:1], ALU.subtract, ALU.mult).then_inc(p_v, 1)
                dve.wait_ge(p_v, 4 * T + 2)
                stat(xn[:, 0, :], pst, p_v)

            def p_stats(T, i):
                dve.wait_ge(p_v, 4 * T + 1 + 2 * i)

            def p_mean():
                aggregate(pst, p_stat)

            def p_third(T):
                dve.wait_ge(p_rstd, 2 * T + 2)
                ge(dve, p_tr, T)
                v.tensor_scalar(xn[:, 1, :], xn[:, 0, :], pst[:, 6:7], prs[:, 1:2], ALU.subtract, ALU.mult).then_inc(p_v, 1)

            def p_fourth(T, m):
                dve.wait_ge(p_tr, T + 1)
                if m is not None:
                    dve.wait_ge(qk_proj, 4 * m + 8)
                    dve.wait_ge(xt_in, 16 * (m + 2))
                v.tensor_scalar(xt[:, bass.ds(T % RING * P, P)], aux_ps[:, 0:P], gbs[:, 0:1], gbs[:, 1:2],
                                ALU.mult, ALU.add).then_inc(p_xt, 1)

            for r in range(2):
                v.memset(kk[DH:P, r, 1, 0, :].bitcast(F32), 0.0)
                v.memset(kk[0:DH, r, 1, 1, :].bitcast(F32), 0.0).then_inc(s_clear, 1)
            v.memset(acc[:, :, :], 0.0).then_inc(s_clear, 1)
            dve.wait_ge(s_clear, 3)
            for r in range(2):
                v.memset(kk[DH:DH + KT, r, 1, 0, :].bitcast(F32), 1.0)
                v.memset(kk[0:KT, r, 1, 1, :].bitcast(F32), 1.0).then_inc(s_clear, 1)
            dve.wait_ge(s_const, 32)
            dve.wait_ge(s_gconst, 1)
            for T in range(AHEAD):
                p_first(T)
                p_stats(T, 0)
                p_mean()
                p_second(T)
                p_stats(T, 1)
                p_mean()
                p_third(T)
                p_fourth(T, None)

            def rope_products(j, t):
                dve.wait_ge(qk_proj, 2 * j + t + 1)
                ge(dve, rope_added, j)
                ge(dve, swap_in, 64 * j)
                ps = (scr0, scr1)[t]
                v.tensor_tensor(rope_s[:, t, :], ps[:, :], cs[:, 1, :], ALU.mult).then_inc(rope_read, 1)
                v.tensor_tensor(rope_c[:, t, :], ps[:, :], cs[:, 0, :], ALU.mult).then_inc(rope_read, 1)

            def lay_max(j, r):
                dve.wait_ge(t_done, j + 1)
                ge(dve, st_mm, 8 * (j - 1))
                for h, half in ((0, slice(DH, P)), (1, slice(0, DH))):
                    v.tensor_tensor(qq[half, r, 1, h, :].rearrange("p (k n) -> p k n", k=KT),
                                    aux_ps[half, 0:P].rearrange("p (o n) -> p o n", o=1).to_broadcast([DH, KT, P]),
                                    cs[half, 2, :].rearrange("p (k n) -> p k n", k=KT), ALU.mult)\
                     .then_inc(mask_done, 1)

            def low_parts(j, r):
                dve.wait_ge(hi_done, 6 * j + 4)
                ge(dve, st_mm, 8 * (j - 1))
                for h in range(2):
                    half = slice(h * DH, (h + 1) * DH)
                    v.tensor_tensor(qq[half, r, 1, h, :], roped[half, 0, :], qq[half, r, 0, h, :].bitcast(F32),
                                    ALU.subtract).then_inc(lo_done, 1)
                dve.wait_ge(hi_done, 6 * j + 6)
                for h in range(2):
                    half = slice(h * DH, (h + 1) * DH)
                    under = slice((1 - h) * DH, (2 - h) * DH)
                    v.tensor_tensor(kk[under, r, 0, h, :], roped[half, 1, :], kk[half, r, 0, h, :].bitcast(F32),
                                    ALU.subtract).then_inc(lo_done, 1)

            def maxima(j, i):
                if i == 0:
                    ge(dve, t_done, j)
                dve.wait_ge(max_mm, 8 * j + i + 1)
                column = i % 2 * DH + i // 2
                v.tensor_reduce(mxp[:, column:column + 1], mx_ps[:, i % 2, :], AX.X, ALU.max).then_inc(max_read, 1)

            def recip(n):
                dve.wait_ge(den8_in, 16 * (n + 1))
                ge(dve, rden_out, 16 * n)
                v.reciprocal(rden8[:, :], den8[:, :]).then_inc(den_recip, 1)

            def add_out(n, b):
                dve.wait_ge(out_mm, n + 1)
                ge(dve, out_read, n)
                here = acc[:, :, :].rearrange("p t d -> p (t d)")[:, bass.ds(b % 2 * N, N)]
                v.tensor_tensor(here, here, scr1[:, :], ALU.add).then_inc(out_read, 1)

            def q_tile(Q, k, at_, num):
                st, tm = stats[:, k, :], tmp[:, k, :]
                xa, xb, xc = pay[:, k, X1:X1 + D], pay[:, k, XS:XS + D], pay[:, k, XH:XH + D]
                rs = rstd_q[:, k, 0:1]
                here = acc[:, :, :].rearrange("p t d -> p (t d)")[:, bass.ds(Q % RING * D, D)]

                def mine(i, ins):
                    ins.then_inc(q_v, 1)
                    dve.wait_ge(q_v, at_(i))

                def stats_of(i):
                    dve.wait_ge(q_v, at_((1, 5, 6)[i]))

                def mean():
                    aggregate(st, q_stat)

                def a0(added):
                    dve.wait_ge(out_read, added)
                    stat(here, st, q_v)

                def a1():
                    dve.wait_ge(q_rstd, num(0) + 1)
                    mine(2, v.tensor_scalar(tm, here, st[:, 6:7], rs, ALU.subtract, ALU.mult))
                    dve.wait_ge(q_in, 16 * (Q + 1) if k == 0 and not isinstance(Q, int) or k == 0 and Q < TILES - BEHIND else 16 * TILES)
                    ge(dve, q_scat, 16 * Q if k == 0 else 16 * (TILES - BEHIND))
                    v.tensor_tensor(xa, xq[:, k, :], tm, ALU.add).then_inc(q_v, 1)
                    v.tensor_copy(here, nothing[:, :]).then_inc(q_v, 1)
                    dve.wait_ge(q_v, at_(4))
                    stat(xa, st, q_v)

                def a2():
                    dve.wait_ge(q_rstd, num(1) + 1)
                    ge(dve, q_xst, Q if k == 0 else 0)
                    v.tensor_scalar(xb, xa, st[:, 6:7], rs, ALU.subtract, ALU.mult).then_inc(q_xs, 1)
                    dve.wait_ge(q_xs, Q + 1)
                    stat(xb, st, q_v)

                def a3():
                    dve.wait_ge(q_rstd, num(2) + 1)
                    mine(7, v.tensor_scalar(xc, xb, st[:, 6:7], rs, ALU.subtract, ALU.mult))

                def copy_xs(transposed):
                    dve.wait_ge(q_xst, transposed)
                    v.tensor_copy(xst[:, k, :], aux_ps[:, 0:P]).then_inc(q_xsc, 1)

                def expert(c, ready):
                    dve.wait_ge(q_aff, ready)
                    af = aux_ps[:, c:c + E]
                    v.tensor_reduce(rt[:, k, 0:1], af, AX.X, ALU.max).then_inc(q_mx, 1)
                    dve.wait_ge(q_mx, Q + 1)
                    mine(8, v.tensor_scalar(ra[:, k, 0, :], af, rt[:, k, 0:1], float(2 * E), ALU.is_lt, ALU.mult))
                    mine(9, v.tensor_tensor(ra[:, k, 0, :], ra[:, k, 0, :], iota8[:, :], ALU.add))
                    mine(10, v.tensor_reduce(rt[:, k, 2:3], ra[:, k, 0, :], AX.X, ALU.min))
                    v.tensor_scalar(oh[:, k, :], iota8[:, :], rt[:, k, 2:3], None, ALU.is_equal).then_inc(q_oh, 1)

                def place(c, ready):
                    dve.wait_ge(q_ea, Q + 1)
                    mine(11, v.tensor_scalar(rt[:, k, 3:4], rt[:, k, 1:2], 1.0, None, ALU.add))
                    mine(12, v.reciprocal(pay[:, k, ALPHA:ALPHA + 1], rt[:, k, 3:4]))
                    v.tensor_scalar(pay[:, k, REST:REST + 1], pay[:, k, ALPHA:ALPHA + 1], -1.0, 1.0, ALU.mult, ALU.add)
                    v.tensor_copy(pay[:, k, TOKEN:TOKEN + 2], token[:, 0:1].to_broadcast([P, 2]))
                    dve.wait_ge(q_rank, ready)
                    mine(13, v.tensor_tensor(ra[:, k, 0, :], base[:, :], aux_ps[:, c:c + E], ALU.add))
                    v.tensor_tensor(base[:, :], base[:, :], aux_ps[:, c + E:c + 2 * E], ALU.add)
                    v.tensor_scalar(token[:, :], token[:, :], float(P), None, ALU.add)
                    mine(14, v.tensor_tensor(ra[:, k, 1, :], ra[:, k, 0, :], oh[:, k, :], ALU.mult))
                    mine(15, v.tensor_reduce(rt[:, k, 4:5], ra[:, k, 1, :], AX.X, ALU.add))
                    v.tensor_copy(pos[:, k:k + 1], rt[:, k, 4:5]).then_inc(q_route, 1)

                return a0, a1, a2, a3, copy_xs, expert, place, stats_of, mean

            def body(m, prep, post):
                first = isinstance(m, int) and m == 0
                last = isinstance(m, int) and m == TILES - 1
                T, Q = m + AHEAD, m - BEHIND
                if post:
                    a0, a1, a2, a3, copy_xs, expert, place, stats_of, mean = q_tile(
                        Q, 0, lambda i: Q * Q_STEPS + i, lambda i: Q * 3 + i)
                n, r = 2 * m, 0

                def both(i, between):
                    if prep and i < 2:
                        p_stats(T, i)
                    if post:
                        stats_of(i)
                    between()
                    if prep and i < 2:
                        p_mean()
                    if post:
                        mean()

                lay_max(n, r)
                maxima(n + 1, 0)
                if prep:
                    p_first(T)
                if post:
                    a0(2 * m - 2)
                both(0, lambda: maxima(n + 1, 1))
                maxima(n + 1, 2)
                if not first:
                    add_out(n - 2, batch(m - 1))
                maxima(n + 1, 3)
                if post:
                    a1()
                if prep:
                    p_second(T)
                both(1, lambda: maxima(n + 1, 4))
                if not first:
                    recip(n - 1)
                maxima(n + 1, 5)
                if not last:
                    rope_products(n + 3, 0)
                if post:
                    a2()
                if prep:
                    p_third(T)
                both(2, lambda: maxima(n + 1, 6))
                if not last:
                    rope_products(n + 3, 1)
                maxima(n + 1, 7)
                if not last:
                    low_parts(n + 2, r)
                if post:
                    a3()
                n, r = 2 * m + 1, 1
                lay_max(n, r)
                if not last:
                    maxima(n + 1, 0)
                    maxima(n + 1, 1)
                if prep:
                    p_fourth(T, m)
                if not last:
                    maxima(n + 1, 2)
                if not first:
                    add_out(n - 2, batch(m - 1))
                if post:
                    copy_xs(Q + 1)
                if not last:
                    maxima(n + 1, 3)
                    maxima(n + 1, 4)
                if post:
                    expert(0, Q + 1)
                recip(n - 1)
                if not last:
                    maxima(n + 1, 5)
                    if not m_is(m, TILES - 2):
                        rope_products(n + 3, 0)
                    maxima(n + 1, 6)
                    if not m_is(m, TILES - 2):
                        rope_products(n + 3, 1)
                if post:
                    place(0, Q + 1)
                if not last:
                    maxima(n + 1, 7)
                    low_parts(n + 2, r)

            rope_products(0, 0)
            rope_products(0, 1)
            low_parts(0, 0)
            rope_products(1, 0)
            rope_products(1, 1)
            for i in range(2 * KT):
                maxima(0, i)
            low_parts(1, 1)
            rope_products(2, 0)
            rope_products(2, 1)
            pairs(dve, body)
            recip(PAIRS - 1)
            add_out(PAIRS - 2, B - 1)
            add_out(PAIRS - 1, B - 1)

            done = TILES - BEHIND
            tiles = [q_tile(done + k, k, lambda i, k=k: done * Q_STEPS + AT[i][k], lambda i, k=k: done * 3 + i * BEHIND + k)
                     for k in range(BEHIND)]
            AT, count = {}, 0
            for part_ in ((1,), (2, 3, 4, 5), (6,), (7,), (8, 9, 10), (11, 12, 13, 14, 15)):
                for k in range(BEHIND):
                    for i in part_:
                        count += 1
                        AT.setdefault(i, {})[k] = count
            for i in range(3):
                for t in tiles:
                    t[i](PAIRS) if i == 0 else t[i]()
                for t in tiles:
                    t[7](i)
                    t[8]()
            for _, _, _, a3, *_ in tiles:
                a3()
            for k, t in enumerate(tiles):
                t[4](done + k + 1)
            for k, t in enumerate(tiles):
                t[5](k * 2 * E, TILES)
            for k, t in enumerate(tiles):
                t[6](k * 2 * E, TILES)

            steps = [0]

            def link(ins):
                steps[0] += 1
                ins.then_inc(r_v, 1)
                dve.wait_ge(r_v, steps[0])

            def over(ap, n):
                return ap.rearrange("p (e o) -> p e o", o=1).to_broadcast([P, ap.shape[-1], n])

            def under(ap, n):
                return ap.rearrange("p (o e) -> p o e", o=1).to_broadcast([P, n, ap.shape[-1]])

            dve.wait_ge(q_route, TILES)
            link(v.tensor_tensor(ex[:, 0, :], base[:, :], first_row[:, :], ALU.subtract))
            link(v.tensor_tensor(cmp[:, :, :], over(ex[:, 0, :], TILES), under(iota128[:, :], E), ALU.is_gt))
            link(v.tensor_reduce(ex[:, 1, :], cmp[:, :, :], AX.X, ALU.add))
            link(v.tensor_copy(ex[:, 2, :], ex[:, 1, :]))
            ea, eb_, s = 2, 3, 1
            while s < E:
                link(v.tensor_tensor(ex[:, eb_, s:], ex[:, ea, s:], ex[:, ea, :E - s], ALU.add))
                link(v.tensor_copy(ex[:, eb_, :s], ex[:, ea, :s]))
                ea, eb_, s = eb_, ea, 2 * s
            link(v.tensor_tensor(ex[:, 4, :], ex[:, ea, :], ex[:, 1, :], ALU.subtract))
            link(v.tensor_scalar(ex[:, 5, :], ex[:, 4, :], -float(P), None, ALU.mult))
            link(v.tensor_tensor(ex[:, 5, :], ex[:, 5, :], first_row[:, :], ALU.add))
            link(v.tensor_tensor(sa[:, 0], under(ex[:, ea, :], SLOTS), over(iotas[:, :], E), ALU.is_gt))
            link(v.tensor_tensor(sa[:, 1], under(ex[:, 4, :], SLOTS), over(iotas[:, :], E), ALU.is_le))
            link(v.tensor_tensor(sa[:, 0], sa[:, 0], sa[:, 1], ALU.mult))
            link(v.tensor_reduce(sl[:, 0, :], sa[:, 0], AX.X, ALU.add))
            link(v.tensor_tensor(sa[:, 1], sa[:, 0], under(iota8[:, :], SLOTS), ALU.mult))
            link(v.tensor_reduce(sl[:, 1, :], sa[:, 1], AX.X, ALU.add))
            v.tensor_copy(texp[:, :], sl[:, 1, :])
            link(v.tensor_tensor(sa[:, 1], sa[:, 0], under(ex[:, 5, :], SLOTS), ALU.mult))
            link(v.tensor_reduce(sl[:, 2, :], sa[:, 1], AX.X, ALU.add))
            link(v.tensor_scalar(sl[:, 3, :], iotas[:, :], float(P), -float(E * CAP), ALU.mult, ALU.add))
            link(v.tensor_tensor(sl[:, 3, :], sl[:, 3, :], sl[:, 0, :], ALU.mult))
            link(v.tensor_tensor(sl[:, 3, :], sl[:, 3, :], sl[:, 2, :], ALU.add))
            link(v.tensor_scalar(sl[:, 3, :], sl[:, 3, :], float(E * CAP), None, ALU.add))
            v.tensor_copy(tdest[:, :], sl[:, 3, :])
            v.tensor_scalar(fpos[:, :], base[:, :], part[:, 0:1], None, ALU.add).then_inc(s_route, 1)
            dve.wait_ge(s_route, 1)
            dve.wait_ge(s_eb, 32)

            def which(t):
                return dve.value_load(texp[0:1, bass.ds(t, 1)], min_val=0, max_val=E - 1)

            def step(t, u, on):
                if on(-2):
                    w = (u - 2) % NB
                    dve.wait_ge(f_rstd, t - 1)
                    v.tensor_scalar(yrow[:, w, :], yrow[:, w, :], fst[:, w, 6:7], frs[:, w, 0:1], ALU.subtract, ALU.mult)\
                     .then_inc(f_norm, 1)
                if on(-1):
                    w = (u - 1) % NB
                    e = which(t - 1)
                    c = turn(t - 1, w)

                    def mine(i, ins):
                        ins.then_inc(f_v, 1)
                        dve.wait_ge(f_v, F_STEPS * (t - 1) + i)

                    y = yrow[:, w, :]
                    dve.wait_ge(fz[w], c + 1)
                    ge(dve, fout[w], 16 * c)
                    v.tensor_tensor(y, z_ps[w], b2s[:, bass.ds(e, 1), :].rearrange("p o f -> p (o f)"), ALU.add)\
                     .then_inc(fzr[w], 1)
                    dve.wait_ge(frest[w], 16 * (c + 1))
                    dve.wait_ge(fzr[w], c + 1)
                    mine(1, v.tensor_tensor(y, y, rest_in[:, w, 0:D], ALU.add))
                    mine(2, v.tensor_scalar(y, y, rest_in[:, w, ALPHA - XS:ALPHA - XS + 1], None, ALU.mult))
                    v.scalar_tensor_tensor(out=y, in0=rest_in[:, w, 0:D], scalar=rest_in[:, w, REST - XS:REST - XS + 1],
                                           in1=y, op0=ALU.mult, op1=ALU.add).then_inc(f_v, 1)
                    v.tensor_copy(tok[:, w:w + 1], rest_in[:, w, TOKEN - XS:TOKEN - XS + 1]).then_inc(f_tok, 1)
                    dve.wait_ge(f_v, F_STEPS * (t - 1) + 3)
                    v.bn_stats(fst[:, w, 0:6], y).then_inc(f_bn, 1)
                if on(2):
                    w = (u + 2) % NB
                    e = which(t + 2)
                    dve.wait_ge(ft[w], turn(t + 2, w) + 1)
                    ge(dve, fh[w], turn(t + 2, w))
                if on(-1):
                    dve.wait_ge(f_bn, t)
                if on(2):
                    w = (u + 2) % NB
                    v.tensor_scalar(xte[:, w, :], bank[w][:, 0:P], egb[:, 0, bass.ds(e, 1)],
                                    egb[:, 1, bass.ds(e, 1)], ALU.mult, ALU.add).then_inc(fxt[w], 1)
                if on(-1):
                    w = (u - 1) % NB
                    v.bn_aggr(fst[:, w, 6:8], fst[:, w, 0:6]).then_inc(f_stat, 1)
                if on(1):
                    w = (u + 1) % NB
                    e = which(t + 1)
                    dve.wait_ge(fh[w], turn(t + 1, w) + 1)
                    v.tensor_tensor(hrow[:, w, :], bank[w][:, :], b1s[:, bass.ds(e, 1), :].rearrange("p o f -> p (o f)"),
                                    ALU.add).then_inc(fhb[w], 1)

            slots(dve, step)

        @block.tensor
        def _(pe):
            t_ = nc.tensor

            def p_turn(T):
                pe.wait_ge(p_v, 4 * T + 4)
                t_.transpose(aux_ps[:, 0:P], xn[:, 1, :], ident[:, :]).then_inc(p_tr, 1)

            pe.wait_ge(s_gconst, 1)
            for T in range(AHEAD):
                ge(pe, p_xt, T)
                p_turn(T)

            def qk_cols(r, part_, kind):
                c0 = part_ * WC + kind * P
                return wqk_st[:, r, c0:c0 + P]

            def project(r, b, kind):
                ps = (scr0, scr1)[kind]
                cols = bass.ds(b % 2 * N, N)
                t_.matmul(ps[:, :], qk_cols(r, 1, kind), xt_hi[:, cols], start=True, stop=False)
                t_.matmul(ps[:, :], qk_cols(r, 0, kind), xt_lo[:, cols], start=False, stop=False)
                t_.matmul(ps[:, :], qk_cols(r, 0, kind), xt_hi[:, cols], start=False, stop=True)\
                  .then_inc(qk_proj, 1)

            def project_q(j, half, r, b):
                pe.wait_ge(qk_in[r], 16 * (half + 1))
                pe.wait_ge(p_lo, KT * b + KT)
                ge(pe, v_read, j - 1)
                ge(pe, rope_read, 4 * j - 2)
                project(r, b, 0)

            def project_k(j, r, b):
                ge(pe, out_read, j - 4)
                ge(pe, rope_read, 4 * j)
                project(r, b, 1)

            def project_v(j, half, r, reads, staged):
                pe.wait_ge(rope_read, reads)
                ge(pe, v_read, j)
                pe.wait_ge(wv_in[r], 16 * (half + 1))
                pe.wait_ge(xt_in, 16 * staged)
                for k in range(KT):
                    ins = t_.matmul(scr0[:, k * P:(k + 1) * P], xt_st[:, k * P:(k + 1) * P], wv_st[:, r, :],
                                    start=True, stop=True)
                ins.then_inc(v_proj, 1)

            def max_scores(j, r, i):
                if i == 0:
                    pe.wait_ge(hi_done, 6 * j + 6)
                    pe.wait_ge(lo_done, 4 * j + 4)
                ge(pe, max_read, 8 * j + i - 1)
                qt, h = i // 2, 1 - i % 2
                t_.matmul(mx_ps[:, i % 2, :], qq[:, r, 0, h, qt * P:(qt + 1) * P], kk[:, r, 0, h, :],
                          start=True, stop=True).then_inc(max_mm, 1)

            def turn_max(j):
                pe.wait_ge(max_read, 8 * j + 8)
                ge(pe, den_copied, j - 1)
                t_.transpose(aux_ps[:, 0:P], mxp[:, :], ident[:, :]).then_inc(t_done, 1)

            def scores(n, r, kt):
                if kt == 0:
                    pe.wait_ge(mask_done, 2 * n + 2)
                for h in range(2):
                    ge(pe, exp_done, 8 * n + 2 * kt + h - 1)
                    ks = slice(kt * P, (kt + 1) * P)
                    t_.matmul(st_ps[:, h, :], kk[:, r, 0, h, ks], qq[:, r, 0, h, :], start=True, stop=False)
                    t_.matmul(st_ps[:, h, :], kk[:, r, 1, h, ks], qq[:, r, 1, h, :], start=False, stop=True)\
                      .then_inc(st_mm, 1)

            def weigh(n, r, kt):
                if kt == 0:
                    pe.wait_ge(v_read, n + 1)
                    ge(pe, o_copied, n)
                pe.wait_ge(exp_done, 8 * n + 2 * kt + 2)
                for h in range(2):
                    ins = t_.matmul(o_ps[h * DH:(h + 1) * DH, :], vals[:, r, kt, h * DH:(h + 1) * DH],
                                    probs[:, r, h, kt, :], start=(kt == 0), stop=(kt == KT - 1))
                if kt == KT - 1:
                    ins.then_inc(av_done, 1)

            def denominators(n, r, laid):
                pe.wait_ge(mask_done, laid)
                pe.wait_ge(pool_sum, 3 * n + 3)
                for h in range(2):
                    ins = t_.matmul(aux_ps[h * DH:(h + 1) * DH, :], ones[:, 0:DH], psums[:, r, h, :], start=True, stop=True)
                ins.then_inc(den_mm, 1)

            def project_out(n, half, r, reads):
                pe.wait_ge(o_norm, n + 1)
                pe.wait_ge(wo_in[r], 16 * (half + 1))
                pe.wait_ge(rope_read, reads)
                ge(pe, out_read, n)
                for k in range(KT):
                    ins = t_.matmul(scr1[:, k * P:(k + 1) * P], onorm[:, k * P:(k + 1) * P], wo_st[:, r, :],
                                    start=True, stop=True)
                ins.then_inc(out_mm, 1)

            def q_turn(Q, k=0):
                pe.wait_ge(q_xs, Q + 1)
                t_.transpose(aux_ps[:, 0:P], pay[:, k, XS:XS + D], ident[:, :]).then_inc(q_xst, 1)

            def q_affinity(Q, k=0, c=0):
                pe.wait_ge(q_xsc, Q + 1)
                t_.matmul(aux_ps[:, c:c + E], xst[:, k, :], cts[:, :], start=True, stop=True).then_inc(q_aff, 1)

            def q_ranks(Q):
                pe.wait_ge(q_oh, Q + 1)
                t_.matmul(aux_ps[:, 0:E], upper[:, :], oh[:, 0, :], start=True, stop=True)
                t_.matmul(aux_ps[:, E:2 * E], ones[:, :], oh[:, 0, :], start=True, stop=True).then_inc(q_rank, 1)

            def body(m, prep, post):
                first = isinstance(m, int) and m == 0
                last = isinstance(m, int) and m == TILES - 1
                T, Q = m + AHEAD, m - BEHIND
                for r in range(2):
                    n = 2 * m + r
                    more = not (last and r)

                    def maxi(*which_):
                        if more:
                            for i in which_:
                                max_scores(n + 1, 1 - r, i)

                    if not r and not first:
                        if post and not m_is(m, BEHIND):
                            pe.wait_ge(q_route, Q)
                        pe.wait_ge(p_xt, T if prep else TILES)
                    turn_max(n)
                    maxi(0, 1)
                    if more:
                        project_v(n + 1, m + r, 1 - r, PAIRS * 4 if last else 4 * n + 10, m + r + 1)
                    scores(n, r, 0)
                    if not (first and not r):
                        denominators(n - 1, 1 - r, 2 * n + 2)
                    maxi(2)
                    scores(n, r, 1)
                    if r and prep:
                        pe.wait_ge(den_copied, n)
                        p_turn(T)
                    weigh(n, r, 0)
                    if not first:
                        project_out(n - 2, m - 1, r, PAIRS * 4 if last else 4 * n + 12)
                    maxi(3)
                    scores(n, r, 2)
                    if r and post:
                        pe.wait_ge(den_copied, n)
                        if prep:
                            pe.wait_ge(p_xt, T + 1)
                        q_turn(Q)
                    weigh(n, r, 1)
                    maxi(4)
                    scores(n, r, 3)
                    if r and post:
                        q_affinity(Q)
                    weigh(n, r, 2)
                    maxi(5)
                    later = not (last or m_is(m, TILES - 2) and r)
                    if later:
                        project_q(n + 3, m + 1 + r, 1 - r, batch(m + 1 + r))
                    maxi(6)
                    if later:
                        project_k(n + 3, 1 - r, batch(m + 1 + r))
                    if r and post:
                        q_ranks(Q)
                    weigh(n, r, 3)
                    maxi(7)

            dve_ready = 5
            pe.wait_ge(s_clear, dve_ready)
            project_q(0, 0, 0, 0)
            project_k(0, 0, 0)
            project_q(1, 0, 1, 0)
            project_k(1, 1, 0)
            project_v(0, 0, 0, 6, 1)
            for i in range(2 * KT):
                max_scores(0, 0, i)
            project_q(2, 1, 0, 0)
            project_k(2, 0, 0)
            pairs(pe, body)
            end = PAIRS - 1
            pe.wait_ge(q_route, TILES - BEHIND)
            denominators(end, 1, 2 * PAIRS)
            project_out(end - 1, TILES - 1, 0, 4 * PAIRS)
            project_out(end, TILES - 1, 1, 4 * PAIRS)

            pe.wait_ge(den_copied, PAIRS)
            done = TILES - BEHIND
            for k in range(BEHIND):
                ge(pe, q_xsc, done + k)
                q_turn(done + k, k)
            pe.wait_ge(q_xsc, TILES)
            for k in range(BEHIND):
                q_affinity(done + k, k, k * 2 * E)
            pe.wait_ge(q_oh, TILES)
            for k in range(BEHIND):
                t_.matmul(aux_ps[:, k * 2 * E:k * 2 * E + E], upper[:, :], oh[:, k, :], start=True, stop=True)
                t_.matmul(aux_ps[:, k * 2 * E + E:(k + 1) * 2 * E], ones[:, :], oh[:, k, :], start=True, stop=True)\
                  .then_inc(q_rank, 1)

            pe.wait_ge(s_ew, 16 * 5)
            pe.wait_ge(s_route, 1)

            def which(t):
                return pe.value_load(texp[0:1, bass.ds(t, 1)], min_val=0, max_val=E - 1)

            def step(t, u, on):
                if on(2):
                    w = (u + 2) % NB
                    pe.wait_ge(fin[w], 16 * (turn(t + 2, w) + 1))
                    ge(pe, fhr[w], turn(t + 2, w))
                    t_.transpose(bank[w][:, 0:P], xh_in[:, w, :], ident[:, :]).then_inc(ft[w], 1)
                if on(1):
                    w = (u + 1) % NB
                    e = which(t + 1)
                    pe.wait_ge(fxt[w], turn(t + 1, w) + 1)
                    t_.matmul(bank[w][:, :], xte[:, w, :], w1s[:, bass.ds(e, 1), :].rearrange("p o f -> p (o f)"),
                              start=True, stop=True).then_inc(fh[w], 1)
                if on(0):
                    pe.wait_ge(fhb[u], turn(t, u) + 1)
                    for c in range(FC):
                        ins = t_.transpose(bank[u][:, c * P:(c + 1) * P], hrow[:, u, c * P:(c + 1) * P], ident[:, :])
                    ins.then_inc(fht[u], 1)
                if on(-1):
                    w = (u - 1) % NB
                    e = which(t - 1)
                    pe.wait_ge(fhr[w], turn(t - 1, w) + 1)
                    ge(pe, fzr[w], turn(t - 1, w))
                    for c in range(FC):
                        ins = t_.matmul(z_ps[w], hcol[:, w, c, :],
                                        w2s[:, bass.ds(e, 1), c, :].rearrange("p o d -> p (o d)"), start=(c == 0), stop=(c == FC - 1))
                    ins.then_inc(fz[w], 1)

            slots(pe, step)


def rope_constants():
    inv_freq = (1.0 / 10000.0 ** (np.arange(0, DH, 2, dtype=np.float32) / np.float32(DH))).astype(np.float32)
    at = np.maximum(np.arange(N) - 1, 0).astype(np.float32)
    angle = at[None, :] * inv_freq[:, None]
    cos, sin = np.cos(angle), np.sin(angle)
    tables = np.zeros((3, P, N), np.float32)
    tables[0] = np.tile(cos, (4, 1))
    tables[1] = np.concatenate([sin, -sin, sin, -sin])
    for k in range(KT):
        tables[2, k, k * P:(k + 1) * P] = -1.0
        tables[2, DH + k, k * P:(k + 1) * P] = -1.0
    return tables


def kernel(L0_attn_x, L0_attn_ln_gamma, L0_attn_ln_beta, L0_attn_w_qkv, L0_attn_w_out, L0_ffn_centroids,
           L0_ffn_ln_g, L0_ffn_ln_b, L0_ffn_w1, L0_ffn_b1, L0_ffn_w2, L0_ffn_b2):
    import concourse.bacc as bacc
    from concourse.bass_utils import run_bass_kernel_spmd

    w = np.asarray(L0_attn_w_qkv).reshape(D, 3, NP, 2, DH)
    arrays = {
        "x": np.asarray(L0_attn_x),
        "wqk": w[:, 0:2].transpose(2, 0, 1, 3, 4).reshape(NP, D, WC),
        "wv": w[:, 2].transpose(1, 0, 2, 3).reshape(NP, D, 2 * DH),
        "wo": np.asarray(L0_attn_w_out).reshape(NP, 2 * DH, D),
        "rope": rope_constants(),
        "gb": np.stack([np.asarray(L0_attn_ln_gamma), np.asarray(L0_attn_ln_beta)], axis=1),
        "cent_t": np.asarray(L0_ffn_centroids).T,
        "eg": np.asarray(L0_ffn_ln_g).T,
        "eb": np.asarray(L0_ffn_ln_b).T,
        "w1t": np.asarray(L0_ffn_w1).transpose(0, 2, 1),
        "b1": np.asarray(L0_ffn_b1),
        "w2t": np.asarray(L0_ffn_w2).transpose(0, 2, 1),
        "b2": np.asarray(L0_ffn_b2),
    }
    arrays = {"in_" + k: np.ascontiguousarray(a) for k, a in arrays.items()}
    nc = bacc.Bacc("TRN2", target_bir_lowering=False, num_devices=1)
    args = [nc.dram_tensor(k, a.shape, mybir.dt.from_np(a.dtype), kind="ExternalInput").ap() for k, a in arrays.items()]
    args.append(nc.dram_tensor("out", (B, N, D), F32, kind="ExternalOutput").ap())
    sandwich_program(nc, *args)
    return run_bass_kernel_spmd(nc, [arrays], core_ids=[0]).results[0]["out"]
```

```python
from contextlib import ExitStack

import numpy as np

import concourse.bass as bass
from concourse import mybir

F32 = mybir.dt.float32
F32R = mybir.dt.float32r
I32 = mybir.dt.int32
U32 = mybir.dt.uint32
ALU = mybir.AluOpType
ACT = mybir.ActivationFunctionType
AX = mybir.AxisListType

B, N, D = 8, 512, 128
H, DH = 16, 64
E, F = 8, 512
P = 128
EPS = 1e-5
SCALE = DH ** -0.5

NP = H // 2
PAIRS = B * NP
KT = N // P
TILES = B * KT
HALF = DH // 2
WC = 2 * P
FC = F // P
AHEAD = KT + 2
BEHIND = 5
RING = 2 * KT

SLOTS = TILES + E - 1
CAP = B * N + P
ROWS = E * CAP + P
XH, XS, X1, ALPHA, REST, TOKEN, ROW = 0, D, 2 * D, 3 * D, 3 * D + 1, 3 * D + 2, 3 * D + 4
NO_TOKEN = 1 << 20


def sandwich_program(nc, x, wqk, wv, wo, rope, gb, cent_t, eg, eb, w1t, b1, w2t, b2, out):
    rows = nc.dram_tensor("rows", (ROWS, ROW), F32, kind="Internal").ap()
    den_row = nc.dram_tensor("den_row", (2, N), F32, kind="Internal").ap()
    rden_row = nc.dram_tensor("rden_row", (2, N), F32, kind="Internal").ap()

    ctx = ExitStack()
    with ctx:
        def sem(name):
            return ctx.enter_context(nc.semaphore(name))

        def keep(name, shape, dt=F32):
            return ctx.enter_context(nc.sbuf_tensor(name, shape, dt))

        acc = keep("acc", [P, RING, D])
        ident = keep("ident", [P, P])
        ones = keep("ones", [P, P])
        upper = keep("upper", [P, P])
        nothing = keep("nothing", [P, D])
        gbs = keep("gbs", [P, 2])
        minus_half = keep("minus_half", [P, 1])
        eps = keep("eps", [P, 1])
        w1s = keep("w1s", [P, E, F])
        w2s = keep("w2s", [P, E, FC, D])
        egb = keep("egb", [P, 2, E])
        cts = keep("cts", [P, E])
        pay = keep("pay", [P, BEHIND, ROW])
        xq = keep("xq", [P, BEHIND, D])
        tmp = keep("tmp", [P, BEHIND, D])
        xst = keep("xst", [P, BEHIND, D])
        stats = keep("stats", [P, BEHIND, 8])
        rstd_q = keep("rstd_q", [P, BEHIND, 2])
        rt = keep("rt", [P, BEHIND, 8])
        ra = keep("ra", [P, BEHIND, 2, E])
        oh = keep("oh", [P, BEHIND, E])
        pos = keep("pos", [P, BEHIND], U32)
        base = keep("base", [P, E])
        token = keep("token", [P, 1])
        iota8 = keep("iota8", [P, E])
        first_row = keep("first_row", [P, E])
        iota128 = keep("iota128", [P, TILES])
        iotas = keep("iotas", [P, SLOTS])
        part = keep("part", [P, 1])

        attn = ExitStack()

        def at(name, shape, dt=F32):
            return attn.enter_context(nc.sbuf_tensor(name, shape, dt))

        probs = at("probs", [P, 2, 2, KT, N])
        psums = at("psums", [P, 2, 2, N])
        xt_hi = at("xt_hi", [P, RING * P], F32R)
        xt_lo = at("xt_lo", [P, RING * P], F32R)
        xt = at("xt", [P, RING * P])
        wqk_all = at("wqk_all", [P, NP, 2 * WC], F32R)
        wqk_st = at("wqk_st", [P, 2, 2 * WC], F32R)
        wv_st = at("wv_st", [P, 2, 2 * DH])
        wo_st = at("wo_st", [P, 2, D])
        xt_st = at("xt_st", [P, N])
        kk = at("kk", [P, 2, 2, 2, N], F32R)
        qq = at("qq", [P, 2, 2, 2, N], F32R)
        vals = at("vals", [P, 2, KT, 2 * DH])
        rope_c = at("rope_c", [P, 2, N])
        rope_s = at("rope_s", [P, 2, N])
        rope_w = at("rope_w", [P, 2, N])
        roped = at("roped", [P, 2, 2, N])
        cs = at("cs", [P, 2, N])
        mxp = at("mxp", [P, KT, P])
        osb = at("osb", [P, 2, N])
        den_sb = at("den_sb", [P, N])
        den8 = at("den8", [P, 8])
        rden8 = at("rden8", [P, 8])
        rden = at("rden", [P, N])
        onorm = at("onorm", [P, N])
        xraw = at("xraw", [P, D])
        xn = at("xn", [P, 2, D])
        pst = at("pst", [P, 8])
        prs = at("prs", [P, 2])
        w_land = psums[:, :].rearrange("p r h (a n) -> p (r h a) n", n=WC)
        attn.close()

        ffn = ExitStack()

        def ff(name, shape, dt=F32):
            return ffn.enter_context(nc.sbuf_tensor(name, shape, dt))

        b1s = ff("b1s", [P, E, F])
        b2s = ff("b2s", [P, E, D])
        cmp = ff("cmp", [P, E, TILES])
        ex = ff("ex", [P, 6, E])
        sa = ff("sa", [P, 2, SLOTS, E])
        sl = ff("sl", [P, 4, SLOTS])
        texp = ff("texp", [P, SLOTS], I32)
        tdest = ff("tdest", [P, SLOTS], I32)
        fill = ff("fill", [P, ROW])
        fpos = ff("fpos", [P, E], U32)
        NB = 4
        xh_in = ff("xh_in", [P, NB, D])
        rest_in = ff("rest_in", [P, NB, ROW - XS])
        tok = ff("tok", [P, NB], U32)
        xte = ff("xte", [P, NB, P])
        hrow = ff("hrow", [P, NB, F])
        hcol = ff("hcol", [P, NB, FC, P])
        yrow = ff("yrow", [P, NB, D])
        fst = ff("fst", [P, NB, 8])
        frs = ff("frs", [P, NB, 2])
        ores = ff("ores", [P, NB, D])
        ffn.close()

        bank = [ctx.enter_context(nc.psum_tensor(f"bank{i}", [P, 512], F32)) for i in range(4)]
        st_ps = ctx.enter_context(nc.psum_tensor("st_ps", [P, 2, N], F32))
        mx_ps = ctx.enter_context(nc.psum_tensor("mx_ps", [P, 2, N], F32))
        scr0, scr1, o_ps, aux_ps = bank
        z_ps = [ps[:, h, 0:D] for ps in (mx_ps, st_ps) for h in range(2)]

        s_const = sem("s_const")
        s_w = [sem(f"s_w{i}") for i in range(NP)]
        s_whi = sem("s_whi")
        s_wlo = sem("s_wlo")
        s_gconst = sem("s_gconst")
        s_gc = sem("s_gc")
        s_clear = sem("s_clear")
        s_ew = sem("s_ew")

        x_in = sem("x_in")
        p_v = sem("p_v")
        p_stat = sem("p_stat")
        p_rstd = sem("p_rstd")
        p_g = sem("p_g")
        p_tr = sem("p_tr")
        p_xt = sem("p_xt")
        p_hi = sem("p_hi")
        p_lo = sem("p_lo")

        qk_in = [sem("qk_in0"), sem("qk_in1")]
        wv_in = [sem("wv_in0"), sem("wv_in1")]
        xt_in = sem("xt_in")
        wo_in = [sem("wo_in0"), sem("wo_in1")]
        qk_proj = sem("qk_proj")
        v_proj = sem("v_proj")
        rope_read = sem("rope_read")
        swap_in = sem("swap_in")
        rope_added = sem("rope_added")
        hi_done = sem("hi_done")
        lo_done = sem("lo_done")
        v_read = sem("v_read")
        max_mm = sem("max_mm")
        max_read = sem("max_read")
        t_done = sem("t_done")
        mask_done = sem("mask_done")
        st_mm = sem("st_mm")
        exp_done = sem("exp_done")
        av_done = sem("av_done")
        o_copied = sem("o_copied")
        pool_sum = sem("pool_sum")
        den_mm = sem("den_mm")
        den_copied = sem("den_copied")
        den_out = sem("den_out")
        den8_in = sem("den8_in")
        den_recip = sem("den_recip")
        rden_out = sem("rden_out")
        rden_in = sem("rden_in")
        o_norm = sem("o_norm")
        out_mm = sem("out_mm")
        out_read = sem("out_read")

        q_in = sem("q_in")
        q_v = sem("q_v")
        q_stat = sem("q_stat")
        q_rstd = sem("q_rstd")
        q_g = sem("q_g")
        q_xs = sem("q_xs")
        q_xst = sem("q_xst")
        q_xsc = sem("q_xsc")
        q_aff = sem("q_aff")
        q_mx = sem("q_mx")
        q_ea = sem("q_ea")
        q_oh = sem("q_oh")
        q_rank = sem("q_rank")
        q_route = sem("q_route")
        q_scat = sem("q_scat")

        s_eb = sem("s_eb")
        s_fpos = sem("s_fpos")
        s_route = sem("s_route")
        r_v = sem("r_v")
        r_p = sem("r_p")
        s_fill = sem("s_fill")
        s_dummy = sem("s_dummy")
        fin = [sem(f"fin{i}") for i in range(NB)]
        frest = [sem(f"frest{i}") for i in range(NB)]
        ft = [sem(f"ft{i}") for i in range(NB)]
        fxt = [sem(f"fxt{i}") for i in range(NB)]
        fh = [sem(f"fh{i}") for i in range(NB)]
        fhb = [sem(f"fhb{i}") for i in range(NB)]
        fht = [sem(f"fht{i}") for i in range(NB)]
        fhr = [sem(f"fhr{i}") for i in range(NB)]
        fz = [sem(f"fz{i}") for i in range(NB)]
        fzr = [sem(f"fzr{i}") for i in range(NB)]
        f_v = sem("f_v")
        f_stat = sem("f_stat")
        f_rstd = sem("f_rstd")
        f_g = sem("f_g")
        f_bn = sem("f_bn")
        f_norm = sem("f_norm")
        f_tok = sem("f_tok")
        f_res = sem("f_res")
        fout = [sem(f"fout{i}") for i in range(NB)]

        Q_STEPS = 15
        F_STEPS = 3

        def ge(eng, s, v):
            if isinstance(v, int) and v <= 0:
                return
            eng.wait_ge(s, v)

        def pairs(eng, body):
            body(0, True, False)
            body(1, True, False)
            with eng.Fori(2, BEHIND) as m:
                body(m, True, False)
            body(BEHIND, True, True)
            with eng.Fori(BEHIND + 1, TILES - AHEAD - 1) as m:
                body(m, True, True)
            body(TILES - AHEAD - 1, True, True)
            with eng.Fori(TILES - AHEAD, TILES - 2) as m:
                body(m, False, True)
            body(TILES - 2, False, True)
            body(TILES - 1, False, True)

        def m_is(m, value):
            return isinstance(m, int) and m == value

        def batch(m):
            return m // KT

        def slots(eng, step, table=None, limit=0):
            def one(t, u, i, known):
                def value(d):
                    if i + d not in known:
                        known[i + d] = eng.value_load(table[0:1, bass.ds(t + d, 1)], min_val=0, max_val=limit)
                    return known[i + d]

                step(t, u % NB, lambda d: not isinstance(t, int) or 0 <= t + d < SLOTS, value)
            end = (SLOTS - NB) // NB
            known = {}
            for t in range(-3, NB + 1):
                one(t, t % NB, t, known)
            with eng.Fori(1, end) as m:
                known = {}
                for i in range(1, NB + 1):
                    one(NB * m + i, i % NB, i, known)
            known = {}
            for t in range(NB * end + 1, SLOTS + 3):
                one(t, t % NB, t, known)

        def turn(t, u):
            return t // NB if isinstance(t, int) else (t - u) // NB

        x_t = x.rearrange("b n d -> (b n) d").rearrange("(t p) d -> t p d", p=P)
        out_rows = out.rearrange("b n d -> (b n) d")

        block = ctx.enter_context(nc.Block())

        @block.sync
        def _(sp):
            def load_x(T):
                ge(sp, p_v, 4 * T - 2)
                src = x_t[T] if isinstance(T, int) else x_t[bass.ds(T, 1)].rearrange("o p d -> p (o d)")
                sp.dma_start(xraw[:, :], src).then_inc(x_in, 16)

            load_x(0)
            sp.dma_start(cs[:, :, :], rope.rearrange("c p n -> p c n")).then_inc(s_const, 16)
            sp.dma_start(gbs[:, :], gb).then_inc(s_const, 16)
            for p in range(NP):
                sp.dma_start(w_land[:, p, :], wqk[p]).then_inc(s_w[p], 16)
            for T in range(1, AHEAD + 1):
                load_x(T)

            def stage_qk(j, r, p):
                ge(sp, qk_proj, 2 * j - 2)
                sp.dma_start(wqk_st[:, r, :].bitcast(F32), wqk_all[:, p, :].bitcast(F32)).then_inc(qk_in[r], 16)

            def stage_v(j, r, p):
                ge(sp, v_proj, j - 1)
                sp.dma_start(wv_st[:, r, :], wv[p]).then_inc(wv_in[r], 16)

            def stage_out(j, r, p):
                ge(sp, out_mm, j - 1)
                sp.dma_start(wo_st[:, r, :], wo[p]).then_inc(wo_in[r], 16)

            def stage_x(m):
                ge(sp, v_proj, 2 * m)
                sp.wait_ge(p_xt, KT * batch(m) + KT)
                sp.dma_start(xt_st[:, :], xt[:, bass.ds(batch(m) % 2 * N, N)]).then_inc(xt_in, 16)

            def swap(j):
                sp.wait_ge(rope_read, 4 * j + 4)
                for q in range(4):
                    to, fr = q * HALF, (q ^ 1) * HALF
                    sp.dma_start(rope_w[to:to + HALF, :, :], rope_s[fr:fr + HALF, :, :]).then_inc(swap_in, 16)

            def den_spread(n):
                sp.wait_ge(den_copied, n + 1)
                for h in range(2):
                    sp.dma_start(den_row[h:h + 1, :], den_sb[h * DH:h * DH + 1, :]).then_inc(den_out, 16)
                sp.wait_ge(den_out, 32 * (n + 1))
                sp.dma_start(den8[:, :], den_row.rearrange("h (p c) -> (h p) c", c=8)).then_inc(den8_in, 16)

            def rden_spread(n):
                ge(sp, o_norm, n)
                sp.wait_ge(den_recip, n + 1)
                sp.dma_start(rden_row.rearrange("h (p c) -> (h p) c", c=8), rden8[:, :]).then_inc(rden_out, 16)
                sp.wait_ge(rden_out, 16 * (n + 1))
                for h in range(2):
                    sp.dma_start(rden[h * DH:(h + 1) * DH, :], rden_row[h:h + 1, :].to_broadcast([DH, N])).then_inc(rden_in, 16)

            def load_q(Q):
                ge(sp, q_stat, 3 * Q - 1)
                sp.dma_start(xq[:, 0, :], x_t[bass.ds(Q, 1)].rearrange("o p d -> p (o d)")).then_inc(q_in, 16)

            def body(m, prep, post):
                first = isinstance(m, int) and m == 0
                last = isinstance(m, int) and m == TILES - 1
                half = NP // 2
                for r in range(2):
                    n = 2 * m + r
                    if r and prep and not m_is(m, TILES - AHEAD - 1):
                        load_x(m + AHEAD + 1)
                    if not r and post:
                        load_q(m - BEHIND)
                    if not m_is(m, TILES - 2) and not last:
                        stage_qk(n + 4, r, (m + 2) % half * 2 + r)
                    if not (first and not r):
                        den_spread(n - 1)
                    if not r and not last:
                        stage_x(m + 1)
                    if not (last or m_is(m, TILES - 2) and r):
                        stage_v(n + 3, 1 - r, (m + 1 + r) % half * 2 + 1 - r)
                        swap(n + 3)
                    if not first:
                        stage_out(n - 1, 1 - r, (m + r - 1) % half * 2 + 1 - r)
                    if not (first and not r):
                        rden_spread(n - 1)

            for n in (0, 1):
                sp.wait_ge(s_whi, n + 1)
                sp.wait_ge(s_wlo, n + 1)
                stage_qk(n, n, n)
            stage_x(0)
            for n in (0, 1):
                stage_v(n, n, n)
                stage_out(n, n, n)
            swap(0)
            for n in (2, 3):
                sp.wait_ge(s_whi, NP)
                sp.wait_ge(s_wlo, NP)
                stage_qk(n, n - 2, n)
                if n == 2:
                    swap(1)
                    stage_v(2, 0, 2)
            swap(2)
            sp.dma_start(w1s[:, :, :], w1t.rearrange("e d f -> d e f")).then_inc(s_ew, 16)
            sp.dma_start(w2s[:, :, :, :], w2t.rearrange("e (c p) d -> p e c d", p=P)).then_inc(s_ew, 16)
            sp.dma_start(egb[:, 0, :], eg).then_inc(s_ew, 16)
            sp.dma_start(egb[:, 1, :], eb).then_inc(s_ew, 16)
            sp.dma_start(cts[:, :], cent_t).then_inc(s_ew, 16)
            pairs(sp, body)
            den_spread(PAIRS - 1)
            stage_out(PAIRS - 1, 1, NP - 1)
            sp.wait_ge(q_stat, 3 * (TILES - BEHIND) - 1)
            for k in range(BEHIND):
                sp.dma_start(xq[:, k, :], x_t[TILES - BEHIND + k]).then_inc(q_in, 16)
            rden_spread(PAIRS - 1)

            sp.wait_ge(out_read, PAIRS)
            sp.dma_start(b1s[:, :, :], b1.rearrange("(o e) f -> o e f", o=1).to_broadcast([P, E, F])).then_inc(s_eb, 16)
            sp.dma_start(b2s[:, :, :], b2.rearrange("(o e) f -> o e f", o=1).to_broadcast([P, E, D])).then_inc(s_eb, 16)
            sp.wait_ge(r_p, 2)
            sp.dma_start(rows[E * CAP:ROWS, :], fill[:, :]).then_inc(s_dummy, 16)
            sp.wait_ge(s_route, 1)
            sp.wait_ge(q_scat, 16 * TILES)
            sp.wait_ge(s_dummy, 16)
            sp.wait_ge(s_fill, 16 * E)

            def step(t, u, on, value):
                if on(3):
                    w = (u + 3) % NB
                    at_row = value(3)
                    ge(sp, ft[w], turn(t + 3, w))
                    sp.dma_start(xh_in[:, w, :], rows[bass.ds(at_row, P), XH:XH + D]).then_inc(fin[w], 16)
                if on(0):
                    at_row = value(0)
                    ge(sp, fout[u], 16 * turn(t, u))
                    sp.dma_start(rest_in[:, u, :], rows[bass.ds(at_row, P), XS:ROW]).then_inc(frest[u], 16)

            slots(sp, step, tdest, E * CAP)
            for u in range(NB):
                sp.wait_ge(fout[u], 16 * ((SLOTS - u + NB - 1) // NB))

        @block.gpsimd
        def _(pool):
            g = nc.gpsimd
            order = [0]

            def link(ins):
                order[0] += 1
                ins.then_inc(s_gc, 1)
                pool.wait_ge(s_gc, order[0])

            g.memset(ident[:, :], 0.0)
            g.memset(upper[:, :], 1.0)
            g.memset(minus_half[:, :], -0.5)
            g.memset(eps[:, :], EPS)
            g.memset(nothing[:, :], 0.0)
            g.memset(mxp[:, :, :], 0.0)
            link(g.memset(ones[:, :], 1.0))
            g.affine_select(out=ident[:, :], in_=ident[:, :], compare_op=ALU.not_equal, fill=1.0,
                            base=0, pattern=[[-1, P]], channel_multiplier=1)
            g.affine_select(out=upper[:, :], in_=upper[:, :], compare_op=ALU.is_gt, fill=0.0,
                            base=0, pattern=[[1, P]], channel_multiplier=-1)

            def iota(ap, step, cm=0, base_=0):
                return g.iota(ap, [[step, ap.shape[-1]]], base=base_, channel_multiplier=cm,
                              allow_small_or_imprecise_dtypes=True)

            iota(iota8[:, :], 1)
            iota(first_row[:, :], CAP)
            iota(base[:, :], CAP)
            iota(iota128[:, :], P)
            iota(iotas[:, :], 1)
            iota(token[:, :], 1, cm=1)
            iota(part[:, :], 1, cm=1).then_inc(s_gconst, 1)

            def rstd(src, dst, stat, own, done, i):
                pool.wait_ge(stat, i + 1)
                g.tensor_tensor(dst, src, eps[:, :], ALU.add).then_inc(own, 1)
                pool.wait_ge(own, i + 1)
                g.tensor_tensor(dst, dst, minus_half[:, :], ALU.pow).then_inc(done, 1)

            def p_rs(T, i):
                rstd(pst[:, 7:8], prs[:, i:i + 1], p_stat, p_g, p_rstd, 2 * T + i)

            def q_rs(Q, i, k=0):
                rstd(stats[:, k, 7:8], rstd_q[:, k, 0:1], q_stat, q_g, q_rstd, Q * 3 + i)

            def low_x(T):
                pool.wait_ge(p_hi, T + 1)
                at_ = bass.ds(T % RING * P, P)
                g.tensor_tensor(xt_lo[:, at_], xt[:, at_], xt_hi[:, at_].bitcast(F32), ALU.subtract).then_inc(p_lo, 1)

            def low_weights(p):
                pool.wait_ge(s_whi, p + 1)
                g.tensor_tensor(wqk_all[:, p, WC:2 * WC], w_land[:, p, :], wqk_all[:, p, 0:WC].bitcast(F32),
                                ALU.subtract).then_inc(s_wlo, 1)

            for T in range(AHEAD):
                p_rs(T, 0)
                p_rs(T, 1)
                low_x(T)
                if T < 2:
                    low_weights(T)
            for p in range(2, NP):
                low_weights(p)

            def add_rope(j, r):
                pool.wait_ge(swap_in, 64 * (j + 1))
                ge(pool, hi_done, 6 * j - 6)
                ge(pool, lo_done, 4 * j - 4)
                g.tensor_tensor(roped[:, r, :, :], rope_c[:, :, :], rope_w[:, :, :], ALU.add).then_inc(rope_added, 1)

            def add_probs(n, r, kt):
                if kt == 1:
                    ge(pool, den_mm, n - 1)
                else:
                    pool.wait_ge(pool_sum, 3 * n + kt - 1)
                pool.wait_ge(exp_done, 8 * n + 2 * kt + 2)
                first = probs[:, r, :, 0, :] if kt == 1 else psums[:, r, :, :]
                g.tensor_tensor(psums[:, r, :, :], first, probs[:, r, :, kt, :], ALU.add).then_inc(pool_sum, 1)

            def normalise(n, r):
                pool.wait_ge(rden_in, 32 * (n + 1))
                pool.wait_ge(o_copied, n + 1)
                ge(pool, out_mm, n)
                g.tensor_tensor(onorm[:, :], osb[:, r, :], rden[:, :], ALU.mult).then_inc(o_norm, 1)

            def scatter(k=0):
                g.indirect_dma_start(out=rows, out_offset=bass.IndirectOffsetOnAxis(ap=pos[:, k:k + 1], axis=0),
                                     in_=pay[:, k, :], in_offset=None).then_inc(q_scat, 16)

            def body(m, prep, post):
                first = isinstance(m, int) and m == 0
                last = isinstance(m, int) and m == TILES - 1
                T, Q = m + AHEAD, m - BEHIND
                for r in range(2):
                    n = 2 * m + r
                    scattered = not r and post and not m_is(m, BEHIND)
                    if scattered:
                        pool.wait_ge(q_route, Q)
                    if not last:
                        add_rope(n + 2, r)
                    else:
                        add_probs(n, r, 1)
                    if scattered:
                        scatter()
                    if not last:
                        add_probs(n, r, 1)
                    if not r and prep:
                        p_rs(T, 0)
                    if not r and post:
                        q_rs(Q, 0)
                    if r and post:
                        q_rs(Q, 2)
                    if not first:
                        normalise(n - 2, r)
                    add_probs(n, r, 2)
                    add_probs(n, r, 3)
                    if r and prep:
                        low_x(T)
                    if not r and prep:
                        p_rs(T, 1)
                    if not r and post:
                        q_rs(Q, 1)

            add_rope(0, 0)
            add_rope(1, 1)
            pairs(pool, body)
            pool.wait_ge(q_route, TILES - BEHIND)
            scatter()
            normalise(PAIRS - 2, 0)
            normalise(PAIRS - 1, 1)
            for i in range(3):
                for k in range(BEHIND):
                    pool.wait_ge(q_stat, 3 * (TILES - BEHIND) + i * BEHIND + k + 1)
                    g.tensor_tensor(rstd_q[:, k, 0:1], stats[:, k, 7:8], eps[:, :], ALU.add).then_inc(q_g, 1)
                    pool.wait_ge(q_g, 3 * (TILES - BEHIND) + i * BEHIND + k + 1)
                    g.tensor_tensor(rstd_q[:, k, 0:1], rstd_q[:, k, 0:1], minus_half[:, :], ALU.pow).then_inc(q_rstd, 1)
            for k in range(BEHIND):
                pool.wait_ge(q_route, TILES - BEHIND + k + 1)
                scatter(k)
            pool.wait_ge(out_read, PAIRS)
            g.memset(fill[:, :], 0.0).then_inc(r_p, 1)
            pool.wait_ge(r_p, 1)
            g.memset(fill[:, TOKEN:TOKEN + 1], float(NO_TOKEN)).then_inc(r_p, 1)
            pool.wait_ge(r_p, 2)
            pool.wait_ge(s_fpos, 1)
            for e in range(E):
                g.indirect_dma_start(out=rows, out_offset=bass.IndirectOffsetOnAxis(ap=fpos[:, e:e + 1], axis=0),
                                     in_=fill[:, :], in_offset=None).then_inc(s_fill, 16)

            def step(t, u, on, value):
                if on(-3):
                    pool.wait_ge(f_res, t - 2)
                    pool.wait_ge(f_tok, t - 2)
                if on(-2):
                    w = (u - 2) % NB
                    pool.wait_ge(f_norm, t - 1)
                    g.tensor_tensor(ores[:, w, :], yrow[:, w, :], rest_in[:, w, X1 - XS:X1 - XS + D], ALU.add)\
                     .then_inc(f_res, 1)
                if on(-3):
                    w = (u - 3) % NB
                    g.indirect_dma_start(out=out_rows, out_offset=bass.IndirectOffsetOnAxis(ap=tok[:, w:w + 1], axis=0),
                                         in_=ores[:, w, :], in_offset=None, bounds_check=B * N - 1,
                                         oob_is_err=False).then_inc(fout[w], 16)
                if on(-1):
                    w = (u - 1) % NB
                    pool.wait_ge(f_stat, t)
                    g.tensor_tensor(frs[:, w, 0:1], fst[:, w, 7:8], eps[:, :], ALU.add).then_inc(f_g, 1)
                    pool.wait_ge(f_g, t)
                    g.tensor_tensor(frs[:, w, 0:1], frs[:, w, 0:1], minus_half[:, :], ALU.pow).then_inc(f_rstd, 1)

            slots(pool, step)

        @block.scalar
        def _(act):
            a = nc.scalar

            def high_weights(p):
                act.wait_ge(s_w[p], 16)
                a.activation(wqk_all[:, p, 0:WC], w_land[:, p, :], ACT.Copy).then_inc(s_whi, 1)

            def high_x(T):
                act.wait_ge(p_xt, T + 1)
                at_ = bass.ds(T % RING * P, P)
                a.activation(xt_hi[:, at_], xt[:, at_], ACT.Copy).then_inc(p_hi, 1)

            for T in range(AHEAD):
                if T < 2:
                    high_weights(T)
                high_x(T)
            for p in range(2, NP):
                high_weights(p)

            def copy_v(j, r):
                act.wait_ge(v_proj, j + 1)
                ge(act, av_done, j - 1)
                a.activation(vals[:, r].rearrange("p k d -> p (k d)"), scr0[:, :], ACT.Copy).then_inc(v_read, 1)

            def copy_o(n, r):
                act.wait_ge(av_done, n + 1)
                ge(act, o_norm, n - 1)
                a.activation(osb[:, r, :], o_ps[:, :], ACT.Copy).then_inc(o_copied, 1)

            def copy_den(n):
                act.wait_ge(den_mm, n + 1)
                ge(act, den_out, 32 * n)
                a.activation(den_sb[:, :], aux_ps[:, :], ACT.Copy).then_inc(den_copied, 1)

            def split_q(j, r):
                act.wait_ge(rope_added, j + 1)
                ge(act, st_mm, 8 * (j - 1))
                for h in range(2):
                    src = roped[h * DH:(h + 1) * DH, r, 0, :]
                    a.activation(qq[0:DH, r, 0, h, :], src, ACT.Copy).then_inc(hi_done, 1)
                    a.activation(qq[DH:P, r, 0, h, :], src, ACT.Copy).then_inc(hi_done, 1)

            def split_k(j, r):
                for h in range(2):
                    half = slice(h * DH, (h + 1) * DH)
                    for c in range(2):
                        ins = a.activation(kk[half, r, c, h, :], roped[half, r, 1, :], ACT.Copy)
                    ins.then_inc(hi_done, 1)

            def lay_max(j, r):
                act.wait_ge(t_done, j + 1)
                ge(act, st_mm, 8 * (j - 1))
                for h, half in ((0, slice(DH, P)), (1, slice(0, DH))):
                    a.activation(qq[half, r, 1, h, :], aux_ps[half, :], ACT.Copy, scale=-1.0).then_inc(mask_done, 1)

            def exps(n, r, kt):
                for h in range(2):
                    act.wait_ge(st_mm, 8 * n + 2 * kt + h + 1)
                    if kt == 0 and h == 0:
                        ge(act, av_done, n - 1)
                        ge(act, pool_sum, 3 * (n - 1))
                    a.activation(probs[:, r, h, kt, :], st_ps[:, h, :], ACT.Exp, scale=SCALE).then_inc(exp_done, 1)

            def exp_alpha(Q, k=0):
                act.wait_ge(q_mx, Q + 1)
                a.activation(rt[:, k, 1:2], rt[:, k, 0:1], ACT.Exp, scale=-1.0).then_inc(q_ea, 1)

            def body(m, prep, post):
                first = isinstance(m, int) and m == 0
                last = isinstance(m, int) and m == TILES - 1
                for r in range(2):
                    n = 2 * m + r
                    more = not (last and r)
                    exps(n, r, 0)
                    if more:
                        copy_v(n + 1, 1 - r)
                    if not (first and not r):
                        copy_o(n - 1, 1 - r)
                    exps(n, r, 1)
                    if not (first and not r):
                        copy_den(n - 1)
                    exps(n, r, 2)
                    exps(n, r, 3)
                    if not last:
                        split_q(n + 2, r)
                    if more:
                        lay_max(n + 1, 1 - r)
                    if not last:
                        split_k(n + 2, r)
                    if r and prep:
                        high_x(m + AHEAD)
                    if r and post:
                        exp_alpha(m - BEHIND)

            split_q(0, 0)
            split_k(0, 0)
            copy_v(0, 0)
            split_q(1, 1)
            split_k(1, 1)
            lay_max(0, 0)
            pairs(act, body)
            copy_o(PAIRS - 1, 1)
            copy_den(PAIRS - 1)
            for k in range(BEHIND):
                exp_alpha(TILES - BEHIND + k, k)

            act.wait_ge(s_ew, 16 * 5)
            act.wait_ge(s_route, 1)

            def step(t, u, on, value):
                if on(2):
                    w2 = (u + 2) % NB
                    e = value(2)
                    act.wait_ge(ft[w2], turn(t + 2, w2) + 1)
                if on(0):
                    act.wait_ge(fht[u], turn(t, u) + 1)
                    ge(act, fz[u], turn(t, u))
                    a.activation(hcol[:, u].rearrange("p c t -> p (c t)"), bank[u][:, :], ACT.Relu).then_inc(fhr[u], 1)
                if on(2):
                    a.activation(xte[:, w2, :], bank[w2][:, 0:P], ACT.Identity, bias=egb[:, 1, bass.ds(e, 1)],
                                 scale=egb[:, 0, bass.ds(e, 1)]).then_inc(fxt[w2], 1)

            slots(act, step, texp, E - 1)

        @block.vector
        def _(dve):
            v = nc.vector

            def stat(src, st, own):
                v.bn_stats(st[:, 0:6], src).then_inc(own, 1)

            def aggregate(st, done):
                v.bn_aggr(st[:, 6:8], st[:, 0:6]).then_inc(done, 1)

            def p_first(T):
                dve.wait_ge(x_in, 16 * (T + 1))
                ge(dve, p_rstd, 2 * T)
                stat(xraw[:, :], pst, p_v)

            def p_second(T):
                dve.wait_ge(p_rstd, 2 * T + 1)
                v.tensor_scalar(xn[:, 0, :], xraw[:, :], pst[:, 6:7], prs[:, 0:1], ALU.subtract, ALU.mult).then_inc(p_v, 1)
                dve.wait_ge(p_v, 4 * T + 2)
                stat(xn[:, 0, :], pst, p_v)

            def p_stats(T, i):
                dve.wait_ge(p_v, 4 * T + 1 + 2 * i)

            def p_mean():
                aggregate(pst, p_stat)

            def p_third(T):
                dve.wait_ge(p_rstd, 2 * T + 2)
                ge(dve, p_tr, T)
                v.tensor_scalar(xn[:, 1, :], xn[:, 0, :], pst[:, 6:7], prs[:, 1:2], ALU.subtract, ALU.mult).then_inc(p_v, 1)

            def p_fourth(T, m):
                dve.wait_ge(p_tr, T + 1)
                if m is not None:
                    dve.wait_ge(qk_proj, 4 * m + 8)
                    dve.wait_ge(xt_in, 16 * (m + 2))
                v.tensor_scalar(xt[:, bass.ds(T % RING * P, P)], aux_ps[:, 0:P], gbs[:, 0:1], gbs[:, 1:2],
                                ALU.mult, ALU.add).then_inc(p_xt, 1)

            for r in range(2):
                v.memset(kk[DH:P, r, 1, 0, :].bitcast(F32), 0.0)
                v.memset(kk[0:DH, r, 1, 1, :].bitcast(F32), 0.0).then_inc(s_clear, 1)
            v.memset(acc[:, :, :], 0.0).then_inc(s_clear, 1)
            dve.wait_ge(s_clear, 3)
            for r in range(2):
                v.memset(kk[DH:DH + 1, r, 1, 0, :].bitcast(F32), 1.0)
                v.memset(kk[0:1, r, 1, 1, :].bitcast(F32), 1.0).then_inc(s_clear, 1)
            dve.wait_ge(s_const, 32)
            dve.wait_ge(s_gconst, 1)
            for T in range(AHEAD):
                p_first(T)
                p_stats(T, 0)
                p_mean()
                p_second(T)
                p_stats(T, 1)
                p_mean()
                p_third(T)
                p_fourth(T, None)

            def rope_products(j, t):
                dve.wait_ge(qk_proj, 2 * j + t + 1)
                ge(dve, rope_added, j)
                ge(dve, swap_in, 64 * j)
                ps = (scr0, scr1)[t]
                v.tensor_tensor(rope_s[:, t, :], ps[:, :], cs[:, 1, :], ALU.mult).then_inc(rope_read, 1)
                v.tensor_tensor(rope_c[:, t, :], ps[:, :], cs[:, 0, :], ALU.mult).then_inc(rope_read, 1)

            def low_parts(j, r):
                dve.wait_ge(hi_done, 6 * j + 4)
                ge(dve, st_mm, 8 * (j - 1))
                for h in range(2):
                    half = slice(h * DH, (h + 1) * DH)
                    v.tensor_tensor(qq[half, r, 1, h, :], roped[half, r, 0, :], qq[half, r, 0, h, :].bitcast(F32),
                                    ALU.subtract).then_inc(lo_done, 1)
                dve.wait_ge(hi_done, 6 * j + 6)
                for h in range(2):
                    half = slice(h * DH, (h + 1) * DH)
                    under = slice((1 - h) * DH, (2 - h) * DH)
                    v.tensor_tensor(kk[under, r, 0, h, :], roped[half, r, 1, :], kk[half, r, 0, h, :].bitcast(F32),
                                    ALU.subtract).then_inc(lo_done, 1)

            def maxima(j, i):
                if i == 0:
                    ge(dve, t_done, j)
                dve.wait_ge(max_mm, 8 * j + i + 1)
                column = i % 2 * DH
                v.tensor_reduce(mxp[:, i // 2, column:column + 1], mx_ps[:, i % 2, :], AX.X, ALU.max).then_inc(max_read, 1)

            def recip(n):
                dve.wait_ge(den8_in, 16 * (n + 1))
                ge(dve, rden_out, 16 * n)
                v.reciprocal(rden8[:, :], den8[:, :]).then_inc(den_recip, 1)

            def add_out(n, b):
                dve.wait_ge(out_mm, n + 1)
                ge(dve, out_read, n)
                here = acc[:, :, :].rearrange("p t d -> p (t d)")[:, bass.ds(b % 2 * N, N)]
                v.tensor_tensor(here, here, scr1[:, :], ALU.add).then_inc(out_read, 1)

            def q_tile(Q, k, at_, num):
                st, tm = stats[:, k, :], tmp[:, k, :]
                xa, xb, xc = pay[:, k, X1:X1 + D], pay[:, k, XS:XS + D], pay[:, k, XH:XH + D]
                rs = rstd_q[:, k, 0:1]
                here = acc[:, :, :].rearrange("p t d -> p (t d)")[:, bass.ds(Q % RING * D, D)]

                def mine(i, ins):
                    ins.then_inc(q_v, 1)
                    dve.wait_ge(q_v, at_(i))

                def stats_of(i):
                    dve.wait_ge(q_v, at_((1, 5, 6)[i]))

                def mean():
                    aggregate(st, q_stat)

                def added(summed):
                    dve.wait_ge(out_read, summed)
                    stat(here, st, q_v)

                def with_x():
                    dve.wait_ge(q_rstd, num(0) + 1)
                    mine(2, v.tensor_scalar(tm, here, st[:, 6:7], rs, ALU.subtract, ALU.mult))
                    dve.wait_ge(q_in, 16 * (Q + 1) if k == 0 and not isinstance(Q, int) or k == 0 and Q < TILES - BEHIND else 16 * TILES)
                    ge(dve, q_scat, 16 * Q if k == 0 else 16 * (TILES - BEHIND))
                    v.tensor_tensor(xa, xq[:, k, :], tm, ALU.add).then_inc(q_v, 1)
                    v.tensor_copy(here, nothing[:, :]).then_inc(q_v, 1)
                    dve.wait_ge(q_v, at_(4))
                    stat(xa, st, q_v)

                def to_xs():
                    dve.wait_ge(q_rstd, num(1) + 1)
                    ge(dve, q_xst, Q if k == 0 else 0)
                    v.tensor_scalar(xb, xa, st[:, 6:7], rs, ALU.subtract, ALU.mult).then_inc(q_xs, 1)
                    dve.wait_ge(q_xs, Q + 1)
                    stat(xb, st, q_v)

                def to_xh():
                    dve.wait_ge(q_rstd, num(2) + 1)
                    mine(7, v.tensor_scalar(xc, xb, st[:, 6:7], rs, ALU.subtract, ALU.mult))

                def copy_xs(transposed, ps=aux_ps):
                    dve.wait_ge(q_xst, transposed)
                    v.tensor_copy(xst[:, k, :], ps[:, 0:P]).then_inc(q_xsc, 1)

                def expert(c, ready):
                    dve.wait_ge(q_aff, ready)
                    af = aux_ps[:, c:c + E]
                    v.tensor_reduce(rt[:, k, 0:1], af, AX.X, ALU.max).then_inc(q_mx, 1)
                    dve.wait_ge(q_mx, Q + 1)
                    mine(8, v.tensor_scalar(ra[:, k, 0, :], af, rt[:, k, 0:1], float(2 * E), ALU.is_lt, ALU.mult))
                    mine(9, v.tensor_tensor(ra[:, k, 0, :], ra[:, k, 0, :], iota8[:, :], ALU.add))
                    mine(10, v.tensor_reduce(rt[:, k, 2:3], ra[:, k, 0, :], AX.X, ALU.min))
                    v.tensor_scalar(oh[:, k, :], iota8[:, :], rt[:, k, 2:3], None, ALU.is_equal).then_inc(q_oh, 1)

                def place(c, ready):
                    dve.wait_ge(q_ea, Q + 1)
                    mine(11, v.tensor_scalar(rt[:, k, 3:4], rt[:, k, 1:2], 1.0, None, ALU.add))
                    mine(12, v.reciprocal(pay[:, k, ALPHA:ALPHA + 1], rt[:, k, 3:4]))
                    v.tensor_scalar(pay[:, k, REST:REST + 1], pay[:, k, ALPHA:ALPHA + 1], -1.0, 1.0, ALU.mult, ALU.add)
                    v.tensor_copy(pay[:, k, TOKEN:TOKEN + 2], token[:, 0:1].to_broadcast([P, 2]))
                    dve.wait_ge(q_rank, ready)
                    mine(13, v.tensor_tensor(ra[:, k, 0, :], base[:, :], aux_ps[:, c:c + E], ALU.add))
                    v.tensor_tensor(base[:, :], base[:, :], aux_ps[:, c + E:c + 2 * E], ALU.add)
                    v.tensor_scalar(token[:, :], token[:, :], float(P), None, ALU.add)
                    mine(14, v.tensor_tensor(ra[:, k, 1, :], ra[:, k, 0, :], oh[:, k, :], ALU.mult))
                    mine(15, v.tensor_reduce(rt[:, k, 4:5], ra[:, k, 1, :], AX.X, ALU.add))
                    v.tensor_copy(pos[:, k:k + 1], rt[:, k, 4:5]).then_inc(q_route, 1)

                return added, with_x, to_xs, to_xh, copy_xs, expert, place, stats_of, mean

            def body(m, prep, post):
                first = isinstance(m, int) and m == 0
                last = isinstance(m, int) and m == TILES - 1
                T, Q = m + AHEAD, m - BEHIND
                if post:
                    added, with_x, to_xs, to_xh, copy_xs, expert, place, stats_of, mean = q_tile(
                        Q, 0, lambda i: Q * Q_STEPS + i, lambda i: Q * 3 + i)
                n, r = 2 * m, 0

                def both(i, between):
                    if prep and i < 2:
                        p_stats(T, i)
                    if post:
                        stats_of(i)
                    between()
                    if prep and i < 2:
                        p_mean()
                    if post:
                        mean()

                low_parts(n + 1, 1 - r)
                if not first and not m_is(m, 1):
                    add_out(n - 3, batch(m - 2))
                for i in range(2):
                    maxima(n + 1, i)
                if prep:
                    p_first(T)
                if post:
                    added(2 * m - 2)
                both(0, lambda: maxima(n + 1, 2))
                for i in range(3, 2 * KT):
                    maxima(n + 1, i)
                if post:
                    with_x()
                if prep:
                    p_second(T)
                both(1, lambda: None if last else rope_products(n + 3, 0))
                if not last:
                    rope_products(n + 3, 1)
                if not first:
                    recip(n - 1)
                n, r = 2 * m + 1, 1
                if not last:
                    low_parts(n + 1, 1 - r)
                if post:
                    to_xs()
                if prep:
                    p_third(T)
                both(2, lambda: None if last else maxima(n + 1, 0))
                if not first:
                    add_out(n - 3, batch(m - 1))
                if not last:
                    for i in range(1, 5):
                        maxima(n + 1, i)
                if prep:
                    p_fourth(T, m)
                if not last:
                    maxima(n + 1, 5)
                    maxima(n + 1, 6)
                if post:
                    copy_xs(Q + 1)
                if not last:
                    maxima(n + 1, 7)
                if post:
                    to_xh()
                if not last:
                    if not m_is(m, TILES - 2):
                        rope_products(n + 3, 0)
                if post:
                    expert(0, Q + 1)
                if not last and not m_is(m, TILES - 2):
                    rope_products(n + 3, 1)
                recip(n - 1)
                if post:
                    place(0, Q + 1)

            rope_products(0, 0)
            rope_products(0, 1)
            low_parts(0, 0)
            rope_products(1, 0)
            rope_products(1, 1)
            for i in range(2 * KT):
                maxima(0, i)
            rope_products(2, 0)
            rope_products(2, 1)
            pairs(dve, body)
            add_out(PAIRS - 3, B - 1)
            recip(PAIRS - 1)
            add_out(PAIRS - 2, B - 1)
            add_out(PAIRS - 1, B - 1)

            done = TILES - BEHIND
            tiles = [q_tile(done + k, k, lambda i, k=k: done * Q_STEPS + AT[i][k], lambda i, k=k: done * 3 + i * BEHIND + k)
                     for k in range(BEHIND)]
            AT, count = {}, 0
            for part_ in ((1,), (2, 3, 4, 5), (6,), (7,), (8, 9, 10), (11, 12, 13, 14, 15)):
                for k in range(BEHIND):
                    for i in part_:
                        count += 1
                        AT.setdefault(i, {})[k] = count
            added, with_x, to_xs, to_xh, copy_xs, expert, place, stats_of, mean = zip(*tiles)
            every = range(BEHIND)
            for i, normalised in enumerate((added, with_x, to_xs)):
                for k in every:
                    normalised[k](*([PAIRS] if i == 0 else []))
                for k in every:
                    stats_of[k](i)
                    mean[k]()
            for k in every:
                to_xh[k]()
            for k in every:
                copy_xs[k](done + k + 1, bank[k % 4])
            for k in every:
                expert[k](k * 2 * E, TILES)
            for k in every:
                place[k](k * 2 * E, TILES)

            steps = [0]

            def link(ins):
                steps[0] += 1
                ins.then_inc(r_v, 1)
                dve.wait_ge(r_v, steps[0])

            def over(ap, n):
                return ap.rearrange("p (e o) -> p e o", o=1).to_broadcast([P, ap.shape[-1], n])

            def under(ap, n):
                return ap.rearrange("p (o e) -> p o e", o=1).to_broadcast([P, n, ap.shape[-1]])

            dve.wait_ge(q_route, TILES)
            v.tensor_scalar(fpos[:, :], base[:, :], part[:, 0:1], None, ALU.add).then_inc(s_fpos, 1)
            link(v.tensor_tensor(ex[:, 0, :], base[:, :], first_row[:, :], ALU.subtract))
            link(v.tensor_tensor(cmp[:, :, :], over(ex[:, 0, :], TILES), under(iota128[:, :], E), ALU.is_gt))
            link(v.tensor_reduce(ex[:, 1, :], cmp[:, :, :], AX.X, ALU.add))
            link(v.tensor_copy(ex[:, 2, :], ex[:, 1, :]))
            ea, eb_, s = 2, 3, 1
            while s < E:
                link(v.tensor_tensor(ex[:, eb_, s:], ex[:, ea, s:], ex[:, ea, :E - s], ALU.add))
                link(v.tensor_copy(ex[:, eb_, :s], ex[:, ea, :s]))
                ea, eb_, s = eb_, ea, 2 * s
            link(v.tensor_tensor(ex[:, 4, :], ex[:, ea, :], ex[:, 1, :], ALU.subtract))
            link(v.tensor_scalar(ex[:, 5, :], ex[:, 4, :], -float(P), None, ALU.mult))
            link(v.tensor_tensor(ex[:, 5, :], ex[:, 5, :], first_row[:, :], ALU.add))
            link(v.tensor_tensor(sa[:, 0], under(ex[:, ea, :], SLOTS), over(iotas[:, :], E), ALU.is_gt))
            link(v.tensor_tensor(sa[:, 1], under(ex[:, 4, :], SLOTS), over(iotas[:, :], E), ALU.is_le))
            link(v.tensor_tensor(sa[:, 0], sa[:, 0], sa[:, 1], ALU.mult))
            link(v.tensor_reduce(sl[:, 0, :], sa[:, 0], AX.X, ALU.add))
            link(v.tensor_tensor(sa[:, 1], sa[:, 0], under(iota8[:, :], SLOTS), ALU.mult))
            link(v.tensor_reduce(sl[:, 1, :], sa[:, 1], AX.X, ALU.add))
            v.tensor_copy(texp[:, :], sl[:, 1, :])
            link(v.tensor_tensor(sa[:, 1], sa[:, 0], under(ex[:, 5, :], SLOTS), ALU.mult))
            link(v.tensor_reduce(sl[:, 2, :], sa[:, 1], AX.X, ALU.add))
            link(v.tensor_scalar(sl[:, 3, :], iotas[:, :], float(P), -float(E * CAP), ALU.mult, ALU.add))
            link(v.tensor_tensor(sl[:, 3, :], sl[:, 3, :], sl[:, 0, :], ALU.mult))
            link(v.tensor_tensor(sl[:, 3, :], sl[:, 3, :], sl[:, 2, :], ALU.add))
            link(v.tensor_scalar(sl[:, 3, :], sl[:, 3, :], float(E * CAP), None, ALU.add))
            v.tensor_copy(tdest[:, :], sl[:, 3, :]).then_inc(s_route, 1)
            dve.wait_ge(s_route, 1)
            dve.wait_ge(s_eb, 32)

            def step(t, u, on, value):
                if on(1):
                    w = (u + 1) % NB
                    e = value(1)
                    dve.wait_ge(fh[w], turn(t + 1, w) + 1)
                    v.tensor_tensor(hrow[:, w, :], bank[w][:, :], b1s[:, bass.ds(e, 1), :].rearrange("p o f -> p (o f)"),
                                    ALU.add).then_inc(fhb[w], 1)
                if on(-2):
                    w = (u - 2) % NB
                    dve.wait_ge(f_rstd, t - 1)
                    v.tensor_scalar(yrow[:, w, :], yrow[:, w, :], fst[:, w, 6:7], frs[:, w, 0:1], ALU.subtract, ALU.mult)\
                     .then_inc(f_norm, 1)
                if on(-1):
                    w = (u - 1) % NB
                    e = value(-1)
                    c = turn(t - 1, w)

                    def mine(i, ins):
                        ins.then_inc(f_v, 1)
                        dve.wait_ge(f_v, F_STEPS * (t - 1) + i)

                    y = yrow[:, w, :]
                    dve.wait_ge(fz[w], c + 1)
                    ge(dve, fout[w], 16 * c)
                    v.tensor_tensor(y, z_ps[w], b2s[:, bass.ds(e, 1), :].rearrange("p o f -> p (o f)"), ALU.add)\
                     .then_inc(fzr[w], 1)
                    dve.wait_ge(frest[w], 16 * (c + 1))
                    dve.wait_ge(fzr[w], c + 1)
                    mine(1, v.tensor_tensor(y, y, rest_in[:, w, 0:D], ALU.add))
                    mine(2, v.tensor_scalar(y, y, rest_in[:, w, ALPHA - XS:ALPHA - XS + 1], None, ALU.mult))
                    mine(3, v.scalar_tensor_tensor(out=y, in0=rest_in[:, w, 0:D], scalar=rest_in[:, w, REST - XS:REST - XS + 1],
                                                   in1=y, op0=ALU.mult, op1=ALU.add))
                    v.bn_stats(fst[:, w, 0:6], y).then_inc(f_bn, 1)
                    dve.wait_ge(f_bn, t)
                    v.tensor_copy(tok[:, w:w + 1], rest_in[:, w, TOKEN - XS:TOKEN - XS + 1]).then_inc(f_tok, 1)
                    v.bn_aggr(fst[:, w, 6:8], fst[:, w, 0:6]).then_inc(f_stat, 1)

            slots(dve, step, texp, E - 1)

        @block.tensor
        def _(pe):
            t_ = nc.tensor

            def p_turn(T):
                pe.wait_ge(p_v, 4 * T + 4)
                t_.transpose(aux_ps[:, 0:P], xn[:, 1, :], ident[:, :]).then_inc(p_tr, 1)

            pe.wait_ge(s_gconst, 1)
            for T in range(AHEAD):
                ge(pe, p_xt, T)
                p_turn(T)

            def qk_cols(r, part_, kind):
                c0 = part_ * WC + kind * P
                return wqk_st[:, r, c0:c0 + P]

            def project(r, b, kind):
                ps = (scr0, scr1)[kind]
                cols = bass.ds(b % 2 * N, N)
                t_.matmul(ps[:, :], qk_cols(r, 1, kind), xt_hi[:, cols], start=True, stop=False)
                t_.matmul(ps[:, :], qk_cols(r, 0, kind), xt_lo[:, cols], start=False, stop=False)
                t_.matmul(ps[:, :], qk_cols(r, 0, kind), xt_hi[:, cols], start=False, stop=True)\
                  .then_inc(qk_proj, 1)

            def project_q(j, half, r, b):
                pe.wait_ge(qk_in[r], 16 * (half + 1))
                pe.wait_ge(p_lo, KT * b + KT)
                ge(pe, v_read, j - 1)
                ge(pe, rope_read, 4 * j - 2)
                project(r, b, 0)

            def project_k(j, r, b):
                ge(pe, out_read, j - 5)
                ge(pe, rope_read, 4 * j)
                project(r, b, 1)

            def project_v(j, half, r, reads, staged):
                pe.wait_ge(rope_read, reads)
                ge(pe, v_read, j)
                pe.wait_ge(wv_in[r], 16 * (half + 1))
                pe.wait_ge(xt_in, 16 * staged)
                for k in range(KT):
                    ins = t_.matmul(scr0[:, k * P:(k + 1) * P], xt_st[:, k * P:(k + 1) * P], wv_st[:, r, :],
                                    start=True, stop=True)
                ins.then_inc(v_proj, 1)

            def max_scores(j, r, i):
                if i == 0:
                    pe.wait_ge(hi_done, 6 * j + 6)
                    pe.wait_ge(lo_done, 4 * j + 4)
                ge(pe, max_read, 8 * j + i - 1)
                qt, h = i // 2, 1 - i % 2
                t_.matmul(mx_ps[:, i % 2, :], qq[:, r, 0, h, qt * P:(qt + 1) * P], kk[:, r, 0, h, :],
                          start=True, stop=True).then_inc(max_mm, 1)

            def turn_max(j):
                pe.wait_ge(max_read, 8 * j + 8)
                ge(pe, den_copied, j - 1)
                for k in range(KT):
                    ins = t_.transpose(aux_ps[:, k * P:(k + 1) * P], mxp[:, k, :], ident[:, :])
                ins.then_inc(t_done, 1)

            def scores(n, r, kt):
                if kt == 0:
                    pe.wait_ge(mask_done, 2 * n + 2)
                for h in range(2):
                    ge(pe, exp_done, 8 * n + 2 * kt + h - 1)
                    ks = slice(kt * P, (kt + 1) * P)
                    t_.matmul(st_ps[:, h, :], kk[:, r, 0, h, ks], qq[:, r, 0, h, :], start=True, stop=False)
                    t_.matmul(st_ps[:, h, :], kk[:, r, 1, h, ks], qq[:, r, 1, h, :], start=False, stop=True)\
                      .then_inc(st_mm, 1)

            def weigh(n, r, kt):
                if kt == 0:
                    pe.wait_ge(v_read, n + 1)
                    ge(pe, o_copied, n)
                pe.wait_ge(exp_done, 8 * n + 2 * kt + 2)
                for h in range(2):
                    ins = t_.matmul(o_ps[h * DH:(h + 1) * DH, :], vals[:, r, kt, h * DH:(h + 1) * DH],
                                    probs[:, r, h, kt, :], start=(kt == 0), stop=(kt == KT - 1))
                if kt == KT - 1:
                    ins.then_inc(av_done, 1)

            def denominators(n, r, laid):
                pe.wait_ge(mask_done, laid)
                pe.wait_ge(pool_sum, 3 * n + 3)
                for h in range(2):
                    ins = t_.matmul(aux_ps[h * DH:(h + 1) * DH, :], ones[:, 0:DH], psums[:, r, h, :], start=True, stop=True)
                ins.then_inc(den_mm, 1)

            def project_out(n, half, r, reads):
                pe.wait_ge(o_norm, n + 1)
                pe.wait_ge(wo_in[r], 16 * (half + 1))
                pe.wait_ge(rope_read, reads)
                ge(pe, out_read, n)
                for k in range(KT):
                    ins = t_.matmul(scr1[:, k * P:(k + 1) * P], onorm[:, k * P:(k + 1) * P], wo_st[:, r, :],
                                    start=True, stop=True)
                ins.then_inc(out_mm, 1)

            def q_turn(Q, k=0, ps=aux_ps):
                pe.wait_ge(q_xs, Q + 1)
                t_.transpose(ps[:, 0:P], pay[:, k, XS:XS + D], ident[:, :]).then_inc(q_xst, 1)

            def q_affinity(Q, k=0, c=0):
                pe.wait_ge(q_xsc, Q + 1)
                t_.matmul(aux_ps[:, c:c + E], xst[:, k, :], cts[:, :], start=True, stop=True).then_inc(q_aff, 1)

            def q_ranks(Q):
                pe.wait_ge(q_oh, Q + 1)
                t_.matmul(aux_ps[:, 0:E], upper[:, :], oh[:, 0, :], start=True, stop=True)
                t_.matmul(aux_ps[:, E:2 * E], ones[:, :], oh[:, 0, :], start=True, stop=True).then_inc(q_rank, 1)

            def body(m, prep, post):
                first = isinstance(m, int) and m == 0
                last = isinstance(m, int) and m == TILES - 1
                T, Q = m + AHEAD, m - BEHIND
                for r in range(2):
                    n = 2 * m + r
                    more = not (last and r)

                    def maxi(*which_):
                        if more:
                            for i in which_:
                                max_scores(n + 1, 1 - r, i)

                    later = not (last or m_is(m, TILES - 2) and r)
                    scores(n, r, 0)
                    if more:
                        project_v(n + 1, m + r, 1 - r, PAIRS * 4 if last else 4 * n + 10, m + r + 1)
                    if not first and not (m_is(m, 1) and not r):
                        project_out(n - 3, m + r - 2, 1 - r, PAIRS * 4 if last else 4 * n + 12)
                    scores(n, r, 1)
                    if not (first and not r):
                        if not r and post and not m_is(m, BEHIND):
                            pe.wait_ge(q_route, Q)
                        denominators(n - 1, 1 - r, 2 * n + 2)
                    maxi(0, 1)
                    weigh(n, r, 0)
                    maxi(2, 3)
                    scores(n, r, 2)
                    if r and prep:
                        pe.wait_ge(den_copied, n)
                        p_turn(T)
                    maxi(4, 5)
                    weigh(n, r, 1)
                    if r and post:
                        pe.wait_ge(den_copied, n)
                        if prep:
                            pe.wait_ge(p_xt, T + 1)
                        q_turn(Q)
                    maxi(6)
                    scores(n, r, 3)
                    maxi(7)
                    if later:
                        project_q(n + 3, m + 1 + r, 1 - r, batch(m + 1 + r))
                    if later:
                        project_k(n + 3, 1 - r, batch(m + 1 + r))
                    if more:
                        if r and post:
                            pe.wait_ge(q_xsc, Q + 1)
                        elif r and prep:
                            pe.wait_ge(p_xt, T + 1)
                        turn_max(n + 1)
                    weigh(n, r, 2)
                    if r and post:
                        if more:
                            pe.wait_ge(mask_done, 2 * n + 4)
                        q_affinity(Q)
                    weigh(n, r, 3)
                    if r and post:
                        q_ranks(Q)

            dve_ready = 5
            pe.wait_ge(s_clear, dve_ready)
            project_q(0, 0, 0, 0)
            project_k(0, 0, 0)
            project_q(1, 0, 1, 0)
            project_k(1, 1, 0)
            project_v(0, 0, 0, 6, 1)
            for i in range(2 * KT):
                max_scores(0, 0, i)
            project_q(2, 1, 0, 0)
            project_k(2, 0, 0)
            pe.wait_ge(p_xt, AHEAD)
            turn_max(0)
            pairs(pe, body)
            end = PAIRS - 1
            pe.wait_ge(q_route, TILES - BEHIND)
            project_out(end - 2, TILES - 2, 1, 4 * PAIRS)
            denominators(end, 1, 2 * PAIRS)
            project_out(end - 1, TILES - 1, 0, 4 * PAIRS)
            project_out(end, TILES - 1, 1, 4 * PAIRS)

            pe.wait_ge(den_copied, PAIRS)
            pe.wait_ge(out_read, PAIRS)
            pe.wait_ge(v_read, PAIRS)
            pe.wait_ge(o_copied, PAIRS)
            done = TILES - BEHIND
            for k in range(BEHIND):
                if k >= 4:
                    pe.wait_ge(q_xsc, done + k - 3)
                q_turn(done + k, k, bank[k % 4])
            pe.wait_ge(q_xsc, TILES)
            for k in range(BEHIND):
                q_affinity(done + k, k, k * 2 * E)
            pe.wait_ge(q_oh, TILES)
            for k in range(BEHIND):
                t_.matmul(aux_ps[:, k * 2 * E:k * 2 * E + E], upper[:, :], oh[:, k, :], start=True, stop=True)
                t_.matmul(aux_ps[:, k * 2 * E + E:(k + 1) * 2 * E], ones[:, :], oh[:, k, :], start=True, stop=True)\
                  .then_inc(q_rank, 1)

            pe.wait_ge(s_ew, 16 * 5)
            pe.wait_ge(s_route, 1)

            def step(t, u, on, value):
                if on(2):
                    w = (u + 2) % NB
                    pe.wait_ge(fin[w], 16 * (turn(t + 2, w) + 1))
                    ge(pe, fhr[w], turn(t + 2, w))
                    t_.transpose(bank[w][:, 0:P], xh_in[:, w, :], ident[:, :]).then_inc(ft[w], 1)
                if on(1):
                    w = (u + 1) % NB
                    e = value(1)
                    pe.wait_ge(fxt[w], turn(t + 1, w) + 1)
                    t_.matmul(bank[w][:, :], xte[:, w, :], w1s[:, bass.ds(e, 1), :].rearrange("p o f -> p (o f)"),
                              start=True, stop=True).then_inc(fh[w], 1)
                if on(0):
                    pe.wait_ge(fhb[u], turn(t, u) + 1)
                    for c in range(FC):
                        ins = t_.transpose(bank[u][:, c * P:(c + 1) * P], hrow[:, u, c * P:(c + 1) * P], ident[:, :])
                    ins.then_inc(fht[u], 1)
                if on(-1):
                    w = (u - 1) % NB
                    e = value(-1)
                    pe.wait_ge(fhr[w], turn(t - 1, w) + 1)
                    ge(pe, fzr[w], turn(t - 1, w))
                    for c in range(FC):
                        ins = t_.matmul(z_ps[w], hcol[:, w, c, :],
                                        w2s[:, bass.ds(e, 1), c, :].rearrange("p o d -> p (o d)"), start=(c == 0), stop=(c == FC - 1))
                    ins.then_inc(fz[w], 1)

            slots(pe, step, texp, E - 1)


def rope_constants():
    inv_freq = (1.0 / 10000.0 ** (np.arange(0, DH, 2, dtype=np.float32) / np.float32(DH))).astype(np.float32)
    at = np.maximum(np.arange(N) - 1, 0).astype(np.float32)
    angle = at[None, :] * inv_freq[:, None]
    cos, sin = np.cos(angle), np.sin(angle)
    tables = np.zeros((2, P, N), np.float32)
    tables[0] = np.tile(cos, (4, 1))
    tables[1] = np.concatenate([sin, -sin, sin, -sin])
    return tables


def kernel(L0_attn_x, L0_attn_ln_gamma, L0_attn_ln_beta, L0_attn_w_qkv, L0_attn_w_out, L0_ffn_centroids,
           L0_ffn_ln_g, L0_ffn_ln_b, L0_ffn_w1, L0_ffn_b1, L0_ffn_w2, L0_ffn_b2):
    import concourse.bacc as bacc
    from concourse.bass_utils import run_bass_kernel_spmd

    w = np.asarray(L0_attn_w_qkv).reshape(D, 3, NP, 2, DH)
    arrays = {
        "x": np.asarray(L0_attn_x),
        "wqk": w[:, 0:2].transpose(2, 0, 1, 3, 4).reshape(NP, D, WC),
        "wv": w[:, 2].transpose(1, 0, 2, 3).reshape(NP, D, 2 * DH),
        "wo": np.asarray(L0_attn_w_out).reshape(NP, 2 * DH, D),
        "rope": rope_constants(),
        "gb": np.stack([np.asarray(L0_attn_ln_gamma), np.asarray(L0_attn_ln_beta)], axis=1),
        "cent_t": np.asarray(L0_ffn_centroids).T,
        "eg": np.asarray(L0_ffn_ln_g).T,
        "eb": np.asarray(L0_ffn_ln_b).T,
        "w1t": np.asarray(L0_ffn_w1).transpose(0, 2, 1),
        "b1": np.asarray(L0_ffn_b1),
        "w2t": np.asarray(L0_ffn_w2).transpose(0, 2, 1),
        "b2": np.asarray(L0_ffn_b2),
    }
    arrays = {"in_" + k: np.ascontiguousarray(a) for k, a in arrays.items()}
    nc = bacc.Bacc("TRN2", target_bir_lowering=False, num_devices=1)
    args = [nc.dram_tensor(k, a.shape, mybir.dt.from_np(a.dtype), kind="ExternalInput").ap() for k, a in arrays.items()]
    args.append(nc.dram_tensor("out", (B, N, D), F32, kind="ExternalOutput").ap())
    sandwich_program(nc, *args)
    return run_bass_kernel_spmd(nc, [arrays], core_ids=[0]).results[0]["out"]
```
